# Optimizing a Trainium2 kernel written in Bass

```python
import numpy as np
import jax
import jax.numpy as jnp

def _softmax(x, axis=-1):
    return jax.nn.softmax(x, axis=axis)

def _gelu(x):
    return jax.nn.gelu(x, approximate=True)

def _silu(x):
    return jax.nn.silu(x)

def _sigmoid(x):
    return jax.nn.sigmoid(x)

def _layernorm(x, axis=-1, eps=1e-05):
    m = jnp.mean(x, axis=axis, keepdims=True)
    v = jnp.var(x, axis=axis, keepdims=True)
    return (x - m) / jnp.sqrt(v + eps)

def _scatter_add(tgt, idx, src, axis=0):
    return tgt.at[idx].add(src)

def _segment_sum(src, seg, n):
    return jax.ops.segment_sum(src, seg, n)
kernel_name = 'mk_conv_seq_d1_conv_nhwc128_r2_d59a15'

def setup_inputs(seed: int=0):
    np.random.seed(seed)
    _w = jnp.asarray

    def _rec_inputs():
        import jax
        import jax.numpy as jnp
        _gk = jax.random.key(seed)
        x = -0.000125 + 0.9999 * jax.random.normal(jax.random.fold_in(_gk, 1), (32, 32, 32, 64), jnp.float32)
        return x
    x = _rec_inputs()

    def _L0_conv_setup():
        import jax, jax.numpy as jnp
        import numpy as np
        W_DIM = 8
        SHIFT = 4
        HEADS = 4

        def _rel_pos_index(w):
            coords = np.stack(np.meshgrid(np.arange(w), np.arange(w), indexing='ij'))
            flat = coords.reshape(2, -1)
            rel = flat[:, :, None] - flat[:, None, :]
            rel = rel.transpose(1, 2, 0) + (w - 1)
            return rel[..., 0] * (2 * w - 1) + rel[..., 1]

        def _shift_mask(H, W, w, s):
            img = np.zeros((H, W), dtype=np.int32)
            cnt = 0
            for hs in (slice(0, -w), slice(-w, -s), slice(-s, None)):
                for ws in (slice(0, -w), slice(-w, -s), slice(-s, None)):
                    img[hs, ws] = cnt
                    cnt += 1
            win = img.reshape(H // w, w, W // w, w).transpose(0, 2, 1, 3).reshape(-1, w * w)
            diff = win[:, None, :] - win[:, :, None]
            return np.where(diff != 0, -1000000000.0, 0.0).astype(np.float32)

        def _ln(x, g, b):
            mu = x.mean(-1, keepdims=True)
            var = x.var(-1, keepdims=True)
            return (x - mu) / jnp.sqrt(var + 1e-05) * g + b

        def _window_partition(x, w):
            B, H, W, C = x.shape
            x = x.reshape(B, H // w, w, W // w, w, C).transpose(0, 1, 3, 2, 4, 5)
            return x.reshape(-1, w * w, C)

        def _window_reverse(win, w, B, H, W):
            C = win.shape[-1]
            x = win.reshape(B, H // w, W // w, w, w, C).transpose(0, 1, 3, 2, 4, 5)
            return x.reshape(B, H, W, C)
        key = jax.random.key(seed)
        ks = jax.random.split(key, 6)
        B, H, W, C = (32, 32, 32, 64)
        d_ff = 4 * C
        return {'x': jax.random.normal(ks[0], (B, H, W, C), jnp.float32), 'ln1_g': jnp.ones((C,), jnp.float32), 'ln1_b': jnp.zeros((C,), jnp.float32), 'qkv_w': jax.random.normal(ks[1], (C, 3 * C), jnp.float32) * 0.02, 'qkv_b': jnp.zeros((3 * C,), jnp.float32), 'proj_w': jax.random.normal(ks[2], (C, C), jnp.float32) * 0.02, 'proj_b': jnp.zeros((C,), jnp.float32), 'rpb': jax.random.normal(ks[3], ((2 * W_DIM - 1) ** 2, HEADS), jnp.float32) * 0.02, 'ln2_g': jnp.ones((C,), jnp.float32), 'ln2_b': jnp.zeros((C,), jnp.float32), 'fc1_w': jax.random.normal(ks[4], (C, d_ff), jnp.float32) * 0.02, 'fc1_b': jnp.zeros((d_ff,), jnp.float32), 'fc2_w': jax.random.normal(ks[5], (d_ff, C), jnp.float32) * 0.02, 'fc2_b': jnp.zeros((C,), jnp.float32)}
    _L0_conv_all = _L0_conv_setup()
    _L0_conv_in = {k: v for k, v in _L0_conv_all.items() if k in ('ln1_g', 'ln1_b', 'qkv_w', 'qkv_b', 'proj_w', 'proj_b', 'rpb', 'ln2_g', 'ln2_b', 'fc1_w', 'fc1_b', 'fc2_w', 'fc2_b')}
    del _L0_conv_all
    return {'x': x, 'L0_conv_ln1_g': _L0_conv_in['ln1_g'], 'L0_conv_ln1_b': _L0_conv_in['ln1_b'], 'L0_conv_qkv_w': _L0_conv_in['qkv_w'], 'L0_conv_qkv_b': _L0_conv_in['qkv_b'], 'L0_conv_proj_w': _L0_conv_in['proj_w'], 'L0_conv_proj_b': _L0_conv_in['proj_b'], 'L0_conv_rpb': _L0_conv_in['rpb'], 'L0_conv_ln2_g': _L0_conv_in['ln2_g'], 'L0_conv_ln2_b': _L0_conv_in['ln2_b'], 'L0_conv_fc1_w': _L0_conv_in['fc1_w'], 'L0_conv_fc1_b': _L0_conv_in['fc1_b'], 'L0_conv_fc2_w': _L0_conv_in['fc2_w'], 'L0_conv_fc2_b': _L0_conv_in['fc2_b']}

def reference(x, L0_conv_ln1_g, L0_conv_ln1_b, L0_conv_qkv_w, L0_conv_qkv_b, L0_conv_proj_w, L0_conv_proj_b, L0_conv_rpb, L0_conv_ln2_g, L0_conv_ln2_b, L0_conv_fc1_w, L0_conv_fc1_b, L0_conv_fc2_w, L0_conv_fc2_b):
    import jax
    import jax.numpy as jnp

    def _L0_conv_ref(x, ln1_g, ln1_b, qkv_w, qkv_b, proj_w, proj_b, rpb, ln2_g, ln2_b, fc1_w, fc1_b, fc2_w, fc2_b):
        import jax, jax.numpy as jnp
        import numpy as np
        W_DIM = 8
        SHIFT = 4
        HEADS = 4

        def _rel_pos_index(w):
            coords = np.stack(np.meshgrid(np.arange(w), np.arange(w), indexing='ij'))
            flat = coords.reshape(2, -1)
            rel = flat[:, :, None] - flat[:, None, :]
            rel = rel.transpose(1, 2, 0) + (w - 1)
            return rel[..., 0] * (2 * w - 1) + rel[..., 1]

        def _shift_mask(H, W, w, s):
            img = np.zeros((H, W), dtype=np.int32)
            cnt = 0
            for hs in (slice(0, -w), slice(-w, -s), slice(-s, None)):
                for ws in (slice(0, -w), slice(-w, -s), slice(-s, None)):
                    img[hs, ws] = cnt
                    cnt += 1
            win = img.reshape(H // w, w, W // w, w).transpose(0, 2, 1, 3).reshape(-1, w * w)
            diff = win[:, None, :] - win[:, :, None]
            return np.where(diff != 0, -1000000000.0, 0.0).astype(np.float32)

        def _ln(x, g, b):
            mu = x.mean(-1, keepdims=True)
            var = x.var(-1, keepdims=True)
            return (x - mu) / jnp.sqrt(var + 1e-05) * g + b

        def _window_partition(x, w):
            B, H, W, C = x.shape
            x = x.reshape(B, H // w, w, W // w, w, C).transpose(0, 1, 3, 2, 4, 5)
            return x.reshape(-1, w * w, C)

        def _window_reverse(win, w, B, H, W):
            C = win.shape[-1]
            x = win.reshape(B, H // w, W // w, w, w, C).transpose(0, 1, 3, 2, 4, 5)
            return x.reshape(B, H, W, C)
        B, H, W, C = x.shape
        w, s, nh = (W_DIM, SHIFT, HEADS)
        hd = C // nh
        N = w * w
        nW = H // w * (W // w)
        h = _ln(x, ln1_g, ln1_b)
        h = jnp.roll(h, (-s, -s), axis=(1, 2))
        win = _window_partition(h, w)
        qkv = win @ qkv_w + qkv_b
        q, k, v = jnp.split(qkv, 3, axis=-1)
        nB = win.shape[0]
        q = q.reshape(nB, N, nh, hd)
        k = k.reshape(nB, N, nh, hd)
        v = v.reshape(nB, N, nh, hd)
        attn = jnp.einsum('bnhd,bmhd->bhnm', q, k) * hd ** (-0.5)
        bias = rpb[jnp.asarray(_rel_pos_index(w))]
        attn = attn + bias.transpose(2, 0, 1)[None]
        mask = jnp.asarray(_shift_mask(H, W, w, s))
        attn = attn.reshape(B, nW, nh, N, N) + mask[None, :, None]
        attn = jax.nn.softmax(attn.reshape(nB, nh, N, N), axis=-1)
        out = jnp.einsum('bhnm,bmhd->bnhd', attn, v).reshape(nB, N, C)
        out = out @ proj_w + proj_b
        out = _window_reverse(out, w, B, H, W)
        out = jnp.roll(out, (s, s), axis=(1, 2))
        x = x + out
        h2 = _ln(x, ln2_g, ln2_b)
        h2 = jax.nn.gelu(h2 @ fc1_w + fc1_b) @ fc2_w + fc2_b
        return x + h2

    def _gn(v, G=32, eps=1e-05):
        B_, H_, W_, C_ = v.shape
        g = v.reshape(B_, H_, W_, G, C_ // G)
        m = jnp.mean(g, axis=(1, 2, 4), keepdims=True)
        s = jnp.var(g, axis=(1, 2, 4), keepdims=True)
        return ((g - m) / jnp.sqrt(s + eps)).reshape(v.shape)

    def _ln_c(v, eps=1e-06):
        m = jnp.mean(v, axis=-1, keepdims=True)
        s = jnp.var(v, axis=-1, keepdims=True)
        return (v - m) / jnp.sqrt(s + eps)

    def _ln_t(v, eps=1e-05):
        m = jnp.mean(v, axis=-1, keepdims=True)
        s = jnp.var(v, axis=-1, keepdims=True)
        return (v - m) / jnp.sqrt(s + eps)

    def _to_tokens(v):
        B_, H_, W_, C_ = v.shape
        return v.reshape(B_, H_ * W_, C_)

    def _from_tokens(t, like):
        return t.reshape(like.shape)
    x = _L0_conv_ref(x, L0_conv_ln1_g, L0_conv_ln1_b, L0_conv_qkv_w, L0_conv_qkv_b, L0_conv_proj_w, L0_conv_proj_b, L0_conv_rpb, L0_conv_ln2_g, L0_conv_ln2_b, L0_conv_fc1_w, L0_conv_fc1_b, L0_conv_fc2_w, L0_conv_fc2_b)
    return x

_drawn_inputs = setup_inputs


def setup_inputs(seed=0):
    import zlib

    import numpy as np

    out = dict(_drawn_inputs(seed))
    spreads = {'L0_conv_ln1_g': (1.0, 0.6),
     'L0_conv_ln1_b': (0.0, 0.8),
     'L0_conv_qkv_b': (0.0, 0.499),
     'L0_conv_proj_b': (0.0, 0.1),
     'L0_conv_ln2_g': (1.0, 0.6),
     'L0_conv_ln2_b': (0.0, 2.0),
     'L0_conv_fc1_b': (0.0, 0.482),
     'L0_conv_fc2_b': (0.0, 0.1)}
    factors = {'L0_conv_qkv_w': 8.0, 'L0_conv_proj_w': 3.509, 'L0_conv_rpb': 8.0}
    for name, (base, spread) in spreads.items():
        noise = np.random.default_rng([zlib.crc32(name.encode()), seed]).standard_normal(out[name].shape)
        drawn = base * np.exp(spread * noise) if base else spread * noise
        out[name] = jnp.asarray(drawn.astype(out[name].dtype))
    for name, factor in factors.items():
        out[name] = (out[name] * factor).astype(out[name].dtype)
    return out
```

```python
from contextlib import ExitStack

import numpy as np

import concourse.bass as bass
from concourse import mybir

F32 = mybir.dt.float32
ACT = mybir.ActivationFunctionType
ALU = mybir.AluOpType
AXX = mybir.AxisListType.X

P = 128
BATCH, SIDE, C = 32, 32, 64
WIN, SHIFT, HEADS = 8, 4, 4
HD = C // HEADS
N = WIN * WIN
FF = 4 * C
GI = P // SIDE
GROUPS = BATCH // GI
ROW = SIDE * C
PIECE = WIN * C
PIECES = ROW // PIECE
QUADS = (SIDE // WIN) * GI
BANK = 512
IMG = 4 * P
EPS = 1e-5
NEG = -1e9


def rel_pos_index():
    at = np.stack(np.meshgrid(np.arange(WIN), np.arange(WIN), indexing="ij")).reshape(2, -1)
    rel = (at[:, :, None] - at[:, None, :]).transpose(1, 2, 0) + (WIN - 1)
    return rel[..., 0] * (2 * WIN - 1) + rel[..., 1]


def shift_masks():
    region = np.zeros((SIDE, SIDE), np.int32)
    parts = (slice(0, -WIN), slice(-WIN, -SHIFT), slice(-SHIFT, None))
    for a, hs in enumerate(parts):
        for b, ws in enumerate(parts):
            region[hs, ws] = 3 * a + b
    k = SIDE // WIN
    win = region.reshape(k, WIN, k, WIN).transpose(0, 2, 1, 3).reshape(k, k, N)
    out = np.zeros((2, N, 2, 2, N), np.float32)
    for v, wi in enumerate((0, k - 1)):
        for wj in range(k):
            differ = win[wi, wj][:, None] != win[wi, wj][None, :]
            out[wj % 2, :, v, wj // 2, :] = np.where(differ, NEG, 0.0)
    return out.reshape(P, 2 * P)


TR_LAG, PV_LAG = 2, 3
SLOTS = QUADS + 4
LN_SLOT = 2


def ln_piece(s, stage, last):
    i, odd = divmod(s - LN_SLOT - stage, 2)
    return i if not (odd or last) and 0 <= i < PIECES else None


def bank_tasks(last):
    tasks = []
    for s in range(SLOTS):
        image, r = divmod(s, 4)
        if s < QUADS - 4:
            tasks.append((s, ("K", "Q", "V", "VT")[r], image + 1))
        elif not last and QUADS - 4 < s < QUADS:
            tasks.append((s, "XT", s - (QUADS - 3)))
            if s == QUADS - 1:
                tasks.append((s, "XT", 3))
        elif not last and s == QUADS:
            tasks.append((s, "K", GI))
        elif not last and s == QUADS + 1:
            tasks += [(s, "Q", GI), (s, "V", GI)]
        elif not last and s == QUADS + 2:
            tasks.append((s, "VT", GI))
        if s >= 7 and s % 4 == 3:
            tasks.append((s, "PROJ", s // 4 - 1))
    tasks += [(SLOTS - 1, "YT", j) for j in range(4)]
    return tasks


FIRST_TASKS = [("XT", 0), ("XT", 1), ("XT", 2), ("XT", 3), ("K", 0), ("Q", 0), ("V", 0), ("VT", 0)]
FIRST_FILLS = len(FIRST_TASKS) // 2
GROUP_FILLS = len(bank_tasks(False)) // 2
LAST_FILLS = len(bank_tasks(True)) // 2
ALL_FILLS = FIRST_FILLS + (GROUPS - 1) * GROUP_FILLS + LAST_FILLS


def build(nc, x_d, g1_d, b1_d, wqkv_d, bqkv_d, wp_d, bp_d, rpb_d, g2_d, b2_d, w1_d, bf1_d, w2_d,
          bf2_d, mask_d, out_d):
    with ExitStack() as ctx:
        def sb(name, *shape):
            return ctx.enter_context(nc.sbuf_tensor(name, [P, *shape], F32))

        def sem(name):
            return ctx.enter_context(nc.semaphore(name))

        bank = [ctx.enter_context(nc.psum_tensor(f"bank{i}", [P, BANK], F32)) for i in range(8)]

        x = sb("x", GROUPS * ROW)
        xn = sb("xn", ROW)
        xT = sb("xT", GI * IMG)
        yT = sb("yT", GI * IMG)
        qT = [sb(f"qT{i}", IMG) for i in range(2)]
        kT = [sb(f"kT{i}", IMG) for i in range(2)]
        vT = [sb(f"vT{i}", IMG) for i in range(2)]
        kX = [sb(f"kX{i}", 2 * HEADS, IMG) for i in range(2)]
        vX = [sb(f"vX{i}", 4 * 2 * HEADS, 2 * HD) for i in range(2)]
        probs = [sb(f"probs{i}", BANK) for i in range(4)]
        probsT = [sb(f"probsT{i}", BANK) for i in range(2)]
        oT = [sb(f"oT{i}", IMG) for i in range(2)]
        rT = [sb(f"rT{i}", P) for i in range(2)]
        recip = [sb(f"recip{i}", P) for i in range(4)]
        negmax = [sb(f"negmax{i}", 8) for i in range(4)]
        rowsum = [sb(f"rowsum{i}", 8) for i in range(4)]
        centred = sb("centred", PIECE)
        squares = sb("squares", PIECE)
        stat_sum = sb("stat_sum", WIN)
        stat_mean = sb("stat_mean", WIN)
        stat_sq = sb("stat_sq", WIN)
        stat_var = sb("stat_var", WIN)
        stat_rstd = sb("stat_rstd", WIN)
        minus_half = sb("minus_half", WIN)
        one_over_c = sb("one_over_c", WIN)
        eps = sb("eps", WIN)
        ident = sb("ident", P)
        bias = [sb(f"bias{i}", BANK) for i in range(2)]
        rpb = sb("rpb", HEADS * N)
        mask = sb("mask", 2 * P)
        wraw = sb("wraw", 3, P)
        wqkv = sb("wqkv", 3, P)
        wproj = sb("wproj", P)
        w1raw = sb("w1raw", 4, P)
        w1 = sb("w1", 4, P)
        w2 = sb("w2", 2, C)
        gain = sb("gain", 2)
        shift = sb("shift", 2)
        bqkv_raw = sb("bqkv_raw", 3)
        bqkv = sb("bqkv", 3)
        bf1_raw = sb("bf1_raw", 2)
        bf1 = sb("bf1", 2)
        bproj = sb("bproj", 1)
        bf2 = sb("bf2", 1)
        xT2 = [sb(f"xT2_{i}", BANK) for i in range(2)]
        hidden = [sb(f"hidden{i}", 4, BANK) for i in range(1)] + [kX[1][:, 0:4, :]]
        y2T = [sb(f"y2T{i}", BANK) for i in range(2)]

        scores = bank[0:2]
        trans = bank[2:4]
        outs = bank[4:6]
        work = bank[6:8]

        x_loaded, params_in = sem("x_loaded"), sem("params_in")
        pool_ready, zeroed = sem("pool_ready"), sem("zeroed")
        params_ready, bias_made = sem("params_ready"), sem("bias_made")
        scores_ready = [sem(f"scores_ready{i}") for i in range(2)]
        scores_taken = [sem(f"scores_taken{i}") for i in range(2)]
        negmax_ready = sem("negmax_ready")
        shifted = [sem("shifted_by_dve"), sem("shifted_by_pool")]
        probs_ready = sem("probs_ready")
        sum_ready, recip_ready = sem("sum_ready"), sem("recip_ready")
        trans_ready = [sem(f"trans_ready{i}") for i in range(2)]
        trans_copied = [sem(f"trans_copied{i}") for i in range(2)]
        outs_ready = [sem(f"outs_ready{i}") for i in range(2)]
        rT_copied = [sem(f"rT_copied{i}") for i in range(2)]
        outs_taken = [sem(f"outs_taken{i}") for i in range(2)]
        work_ready = [sem(f"work_ready{i}") for i in range(2)]
        work_taken = [sem(f"work_taken{i}") for i in range(2)]
        kX_loaded = [sem(f"kX_loaded{i}") for i in range(2)]
        ln_sum, ln_mean, ln_centred = sem("ln_sum"), sem("ln_mean"), sem("ln_centred")
        ln_squares, ln_sq, ln_var = sem("ln_squares"), sem("ln_sq"), sem("ln_var")
        ln_eps, ln_rstd, xn_ready = sem("ln_eps"), sem("ln_rstd"), sem("xn_ready")
        xT2_ready, xT2_copied = sem("xT2_ready"), sem("xT2_copied")
        fc1_ready, gelu_done = sem("fc1_ready"), sem("gelu_done")
        fc2_ready, y2T_copied = sem("fc2_ready"), sem("y2T_copied")
        y2_ready, out_ready, stored = sem("y2_ready"), sem("out_ready"), sem("stored")

        N_PARAMS = 2 * (9 + 3) + 1 + 2 + 1 + 2 * HEADS
        COPIES = SIDE // WIN * 2
        KX_DMAS = 2 * HEADS

        block = ctx.enter_context(nc.Block())

        def group_base(g):
            return FIRST_FILLS + GROUP_FILLS * g

        def tasks_of(g, last):
            return [(s, kind, i, t % 2, group_base(g) + t // 2)
                    for t, (s, kind, i) in enumerate(bank_tasks(last))]

        def rows_of(group_dma, g):
            for a in range(GI):
                for r0, r1, s0 in ((0, SIDE - SHIFT, SHIFT), (SIDE - SHIFT, SIDE, 0)):
                    hbm = group_dma[bass.ds(g * GI + a, 1), s0:s0 + r1 - r0]
                    yield (x[SIDE * a + r0:SIDE * a + r1, bass.ds(g * ROW, ROW)],
                           hbm.rearrange("o r c f -> (o r) (c f)"))

        @block.sync
        def _(sp):
            def load(g):
                for dst, src in rows_of(x_d, g):
                    sp.dma_start(dst, src).then_inc(x_loaded, 16)

            def spread_keys(par, fill):
                for j in range(2 * HEADS):
                    rows = slice(HD * j, HD * (j + 1))
                    sp.dma_start(kX[par][rows, j, :], kT[par][rows, :]).then_inc(kX_loaded[par], 16)

            load(0)
            sp.wait_ge(pool_ready, 1)
            for w in range(2):
                half = slice(C * w, C * (w + 1))
                sp.dma_start(wraw[half, :, half], wqkv_d.rearrange("c (t o) -> c t o", t=3))\
                  .then_inc(params_in, 16)
                sp.dma_start(w1raw[half, 2 * w:2 * w + 2, :], w1_d.rearrange("c (t o) -> c t o", t=2))\
                  .then_inc(params_in, 16)
                sp.dma_start(gain[half, 0:1], g1_d.unsqueeze(1)).then_inc(params_in, 16)
                sp.dma_start(gain[half, 1:2], g2_d.unsqueeze(1)).then_inc(params_in, 16)
                sp.dma_start(shift[half, 0:1], b1_d.unsqueeze(1)).then_inc(params_in, 16)
                sp.dma_start(shift[half, 1:2], b2_d.unsqueeze(1)).then_inc(params_in, 16)
                sp.dma_start(bproj[half, :], bp_d.unsqueeze(1)).then_inc(params_in, 16)
                sp.dma_start(bf2[half, :], bf2_d.unsqueeze(1)).then_inc(params_in, 16)
                sp.dma_start(rpb[half, :], rpb_d).then_inc(params_in, 16)
                for t in range(3):
                    sp.dma_start(bqkv_raw[half, t:t + 1], bqkv_d[C * t:C * (t + 1)].unsqueeze(1))\
                      .then_inc(params_in, 16)
            sp.dma_start(mask[:, :], mask_d).then_inc(params_in, 16)
            for t in range(2):
                sp.dma_start(bf1_raw[:, t:t + 1], bf1_d[P * t:P * (t + 1)].unsqueeze(1))\
                  .then_inc(params_in, 16)
            sp.dma_start(w2[:, :, :], w2_d.rearrange("(t k) c -> k t c", t=2)).then_inc(params_in, 16)
            for h in range(HEADS):
                for p in range(2):
                    at = 2 * HD * h + HD * p
                    sp.dma_start(wproj[at:at + HD, C * p:C * (p + 1)], wp_d[HD * h:HD * (h + 1), :])\
                      .then_inc(params_in, 16)
            sp.wait_ge(zeroed, 2)
            sp.wait_ge(work_taken[0], 3)
            spread_keys(0, 0)

            def group(g, last):
                if not last:
                    sp.wait_ge(x_loaded, 16 * COPIES * (g + 1))
                    load(g + 1)
                for s, kind, i, b, fill in tasks_of(g, last):
                    if kind == "K":
                        sp.wait_ge(work_taken[b], fill + 1)
                        spread_keys(i % 2, g)

            with sp.Fori(0, GROUPS - 1) as g:
                group(g, False)
            group(GROUPS - 1, True)

            with sp.Fori(0, GROUPS) as g:
                sp.wait_ge(out_ready, PIECES * g + PIECES)
                for src, dst in rows_of(out_d, g):
                    sp.dma_start(dst, src).then_inc(stored, 16)
            sp.wait_ge(stored, 16 * COPIES * GROUPS)

        @block.gpsimd
        def _(pool):
            nc.gpsimd.memset(wraw[:, :, :], 0.0)
            nc.gpsimd.memset(w1raw[:, :, :], 0.0)
            nc.gpsimd.memset(wproj[:, :], 0.0)
            nc.gpsimd.memset(minus_half[:, :], -0.5)
            nc.gpsimd.memset(one_over_c[:, :], 1.0 / C)
            nc.gpsimd.memset(eps[:, :], EPS)
            nc.gpsimd.memset(ident[:, :], 0.0).then_inc(pool_ready, 1)
            pool.wait_ge(pool_ready, 1)
            nc.gpsimd.affine_select(out=ident[:, :], in_=ident[:, :], compare_op=ALU.not_equal,
                                    fill=1.0, base=0, pattern=[[-1, P]], channel_multiplier=1)\
              .then_inc(pool_ready, 1)
            nc.gpsimd.memset(kX[1][:, :, :], 0.0).then_inc(zeroed, 1)

            def centre(src, u):
                pool.wait_ge(ln_sum, u + 1)
                nc.gpsimd.tensor_tensor(stat_mean[:, :], stat_sum[:, :], one_over_c[:, :], ALU.mult)\
                  .then_inc(ln_mean, 1)
                pool.wait_ge(ln_mean, u + 1)
                mean = stat_mean[:, :].unsqueeze(2).to_broadcast([P, WIN, C])
                nc.gpsimd.tensor_tensor(centred[:, :].rearrange("q (a f) -> q a f", f=C),
                                        src.rearrange("q (a f) -> q a f", f=C), mean, ALU.add)\
                  .then_inc(ln_centred, 1)

            def scale(parts, u):
                pool.wait_ge(ln_sq, u + 1)
                nc.gpsimd.tensor_tensor(stat_var[:, :], stat_sq[:, :], eps[:, :], ALU.add)\
                  .then_inc(ln_var, 1)
                pool.wait_ge(ln_var, u + 1)
                nc.gpsimd.tensor_tensor(stat_rstd[:, :], stat_var[:, :], minus_half[:, :], ALU.pow)\
                  .then_inc(ln_rstd, 1)
                pool.wait_ge(ln_rstd, u + 1)
                for k, (dst, a0, a1) in enumerate(parts):
                    rstd = stat_rstd[:, a0:a1].unsqueeze(2).to_broadcast([P, a1 - a0, C])
                    last = nc.gpsimd.tensor_tensor(
                        dst, centred[:, a0 * C:a1 * C].rearrange("q (a f) -> q a f", f=C), rstd,
                        ALU.mult)
                last.then_inc(xn_ready, 1)

            xn_v = xn[:, :].rearrange("q (p c w f) -> q p c w f", p=2, c=WIN, w=2)

            def window_parts(i):
                before = (i - 1) % PIECES
                return [(xn_v[:, before // 2, SHIFT:WIN, before % 2, :], 0, SHIFT),
                        (xn_v[:, i // 2, 0:SHIFT, i % 2, :], SHIFT, WIN)]

            for i in range(PIECES):
                centre(x[:, i * PIECE:(i + 1) * PIECE], i)
                scale(window_parts(i), i)

            def group(g, last):
                for s in range(QUADS):
                    if s % 2:
                        pool.wait_ge(negmax_ready, QUADS * g + s + 1)
                        top = negmax[s % 4][:, :].unsqueeze(2).to_broadcast([P, 8, N])
                        e = probs[s % 4][:, :].rearrange("q (a m) -> q a m", m=N)
                        nc.gpsimd.tensor_tensor(e, e, top, ALU.add).then_inc(shifted[1], 1)
                    if (i := ln_piece(s, 2, last)) is not None:
                        scale(window_parts(i), PIECES * (g + 1) + i)
                    if (i := ln_piece(s, 0, last)) is not None:
                        centre(x[:, bass.ds((g + 1) * ROW + i * PIECE, PIECE)], PIECES * (g + 1) + i)

            with pool.Fori(0, GROUPS - 1) as g:
                group(g, False)
            group(GROUPS - 1, True)

            def normalise2(u2, par):
                u = GROUPS * PIECES + u2
                centre(x[:, bass.ds(u2 * PIECE, PIECE)], u)
                if not isinstance(u2, int) or u2 >= 2:
                    pool.wait_ge(xT2_ready, u2 - 1)
                dst = xn[:, par * PIECE:(par + 1) * PIECE].rearrange("q (a f) -> q a f", f=C)
                scale([(dst, 0, WIN)], u)

            for u2 in range(4):
                normalise2(u2, u2 % 2)
            with pool.Fori(2, GROUPS * PIECES // 2) as k:
                normalise2(2 * k, 0)
                normalise2(2 * k + 1, 1)

        @block.vector
        def _(dve):
            def row_sum(src, u):
                if not isinstance(u, int) or u >= 1:
                    dve.wait_ge(ln_centred, u)
                nc.vector.tensor_reduce(stat_sum[:, :], src.rearrange("q (a f) -> q a f", f=C), AXX,
                                        ALU.add, negate=True).then_inc(ln_sum, 1)

            def square_sum(u):
                dve.wait_ge(ln_squares, u + 1)
                nc.vector.tensor_reduce(stat_sq[:, :], squares[:, :].rearrange("q (a f) -> q a f", f=C),
                                        AXX, ALU.add).then_inc(ln_sq, 1)

            nc.vector.memset(kX[0][:, :, :], 0.0)
            nc.vector.memset(vX[0][:, :, :], 0.0)
            nc.vector.memset(vX[1][:, :, :], 0.0).then_inc(zeroed, 1)
            for b in range(2):
                dve.sem_inc(scores_taken[b], 1)
                dve.sem_inc(outs_taken[b], 1)
            dve.wait_ge(x_loaded, 16 * COPIES)
            row_sum(x[:, 0:PIECE], 0)
            dve.wait_ge(params_in, 16 * N_PARAMS)
            for t in range(3):
                nc.vector.tensor_scalar(wqkv[:, t, :], wraw[:, t, :], gain[:, 0:1], None, ALU.mult)
            for t in range(4):
                last = nc.vector.tensor_scalar(w1[:, t, :], w1raw[:, t, :], gain[:, 1:2], None,
                                               ALU.mult)
            last.then_inc(params_ready, 1)
            for v in range(2):
                r = rpb[:, :].rearrange("q (h m) -> q h m", h=HEADS).unsqueeze(2)\
                    .to_broadcast([P, HEADS, 2, N])
                m = mask[:, v * P:(v + 1) * P].rearrange("q (p m) -> q p m", p=2).unsqueeze(1)\
                    .to_broadcast([P, HEADS, 2, N])
                nc.vector.tensor_tensor(bias[v][:, :].rearrange("q (h p m) -> q h p m", h=HEADS, p=2),
                                        r, m, ALU.add).then_inc(bias_made, 1)
            square_sum(0)
            for i in range(1, PIECES):
                row_sum(x[:, i * PIECE:(i + 1) * PIECE], i)
                square_sum(i)
            dve.wait_ge(bias_made, 2)

            def group(g, last):
                tasks = tasks_of(g, last)
                for s in range(SLOTS):
                    if s < QUADS:
                        b, fill = s % 2, (QUADS // 2) * g + s // 2
                        e = probs[s % 4]
                        dve.wait_ge(scores_ready[b], fill + 1)
                        nc.vector.tensor_tensor(e[:, :], scores[b][:, :],
                                                bias[s % 4 == 3][:, :], ALU.add)\
                          .then_inc(scores_taken[b], 1)
                        dve.wait_ge(scores_taken[b], fill + 2)
                        e3 = e[:, :].rearrange("q (a m) -> q a m", m=N)
                        nc.vector.tensor_reduce(negmax[s % 4][:, :], e3, AXX, ALU.max, negate=True)\
                          .then_inc(negmax_ready, 1)
                        if s % 2 == 0:
                            dve.wait_ge(negmax_ready, QUADS * g + s + 1)
                            top = negmax[s % 4][:, :].unsqueeze(2).to_broadcast([P, 8, N])
                            nc.vector.tensor_tensor(e3, e3, top, ALU.add).then_inc(shifted[0], 1)
                    if 1 <= s < QUADS + 1:
                        q = s - 1
                        dve.wait_ge(probs_ready, QUADS * g + q + 1)
                        nc.vector.tensor_reduce(rowsum[q % 4][:, :],
                                                probs[q % 4][:, :].rearrange("q (a m) -> q a m", m=N),
                                                AXX, ALU.add).then_inc(sum_ready, 1)
                        dve.wait_ge(sum_ready, QUADS * g + q + 1)
                        nc.vector.reciprocal(recip[q % 4][:, :].rearrange("q (a d) -> q a d", d=HD),
                                             rowsum[q % 4][:, :].unsqueeze(2)
                                             .to_broadcast([P, 8, HD])).then_inc(recip_ready, 1)
                    if s >= PV_LAG and s - PV_LAG < QUADS:
                        q = s - PV_LAG
                        b, fill = q % 2, (QUADS // 2) * g + q // 2
                        dve.wait_ge(rT_copied[b], fill + 1)
                        nc.vector.tensor_tensor(oT[q // 4 % 2][:, q % 4 * P:(q % 4 + 1) * P],
                                                outs[b][:, 0:P], rT[b][:, :], ALU.mult)\
                          .then_inc(outs_taken[b], 1)
                    if (i := ln_piece(s, 2, last)) is not None:
                        square_sum(PIECES * (g + 1) + i)
                    if (i := ln_piece(s, 0, last)) is not None:
                        if i == 0:
                            dve.wait_ge(x_loaded, 16 * COPIES * (g + 2))
                        row_sum(x[:, bass.ds((g + 1) * ROW + i * PIECE, PIECE)], PIECES * (g + 1) + i)
                    for ts, kind, j, b, fill in tasks:
                        if ts != s or kind != "YT":
                            continue
                        dve.wait_ge(work_ready[b], fill + 1)
                        w, c0 = j // 2, (j % 2) * SHIFT
                        src = work[b][:, :].rearrange("q (c p f) -> q c p f", c=4, p=2)
                        if (w, c0) != (1, SHIFT):
                            col = WIN * w + c0 + SHIFT
                            dst = x[:, bass.ds(g * ROW, ROW)]\
                                .rearrange("q (p c f) -> q c p f", p=2, f=C)[:, col:col + SHIFT]
                            nc.vector.tensor_tensor(dst, src, dst, ALU.add)\
                              .then_inc(work_taken[b], 1)
                            continue
                        for p, col in ((0, 2 * WIN), (1, 0)):
                            dst = x[:, bass.ds(g * ROW + col * C, SHIFT * C)]\
                                .rearrange("q (c f) -> q c f", f=C)
                            done = nc.vector.tensor_tensor(dst, src[:, :, p, :], dst, ALU.add)
                        done.then_inc(work_taken[b], 1)

            with dve.Fori(0, GROUPS - 1) as g:
                group(g, False)
            group(GROUPS - 1, True)
            for b in range(2):
                dve.wait_ge(work_taken[b], ALL_FILLS)

            def step(s, x_in, copy, add):
                if copy:
                    dve.wait_ge(xT2_ready, s + 2)
                    nc.vector.tensor_copy(xT2[(s + 1) % 2 if isinstance(s, int) else x_in][:, :],
                                          bank[0][:, :]).then_inc(xT2_copied, 1)
                if add:
                    dve.wait_ge(y2_ready, s - 1)
                    dst = x[:, bass.ds((s - 2) * PIECE, PIECE)]
                    nc.vector.tensor_tensor(dst, bank[6][:, :], dst, ALU.add).then_inc(out_ready, 1)

            def stats(s):
                u = GROUPS * PIECES + s
                row_sum(x[:, bass.ds(s * PIECE, PIECE)], u)
                square_sum(u)

            S = GROUPS * PIECES
            stats(0)
            for s in range(-1, 4):
                step(s, 0, True, s >= 2)
                stats(s + 2)
            with dve.Fori(2, (S - 4) // 2 + 1) as k:
                for d in range(2):
                    step(2 * k + d, (d + 1) % 2, True, True)
                    stats(2 * k + d + 2)
            for s in range(S - 2, S + 2):
                step(s, 0, s + 1 < S, True)

        @block.scalar
        def _(act):
            def square(u):
                act.wait_ge(ln_centred, u + 1)
                nc.scalar.activation(squares[:, :], centred[:, :], ACT.Square,
                                     scale=float(C) ** -0.5).then_inc(ln_squares, 1)

            def take(kind, i, b, fill):
                act.wait_ge(work_ready[b], fill + 1)
                src, par = work[b], i % 2
                if kind == "XT":
                    p, c0 = i // 2, i % 2 * 4
                    dst = xT[:, :].rearrange("q (i p r c) -> q p c i r", p=2, r=WIN, c=WIN)
                    done = nc.scalar.activation(
                        dst[:, p, c0:c0 + 4],
                        src[:, :].rearrange("q (c i r) -> q c i r", c=4, r=WIN), ACT.Copy)
                elif kind == "Q":
                    done = nc.scalar.activation(qT[par][:, :], src[:, :], ACT.Identity,
                                                bias=bqkv[:, 0:1], scale=float(HD) ** -0.5)
                elif kind == "K":
                    done = nc.scalar.activation(kT[par][:, :], src[:, :], ACT.Identity,
                                                bias=bqkv[:, 1:2])
                elif kind == "V":
                    done = nc.scalar.activation(vT[par][:, :], src[:, :], ACT.Identity,
                                                bias=bqkv[:, 2:3])
                elif kind == "VT":
                    for p in range(2):
                        half = slice(N * p, N * (p + 1))
                        done = nc.scalar.activation(
                            vX[par][half, :, HD * p:HD * (p + 1)],
                            src[half, :].rearrange("q (a d) -> q a d", d=HD), ACT.Copy)
                elif kind == "PROJ":
                    for w in range(2):
                        dst = yT[:, :].rearrange("q (w c i y r) -> q w i y r c", w=2, c=WIN, i=GI,
                                                 y=SIDE // WIN)
                        done = nc.scalar.activation(
                            dst[:, w, i],
                            src[:, :].rearrange("q (y w r c) -> q w y r c", y=SIDE // WIN, w=2,
                                                r=WIN)[:, w],
                            ACT.Identity, bias=bproj[:, 0:1])
                done.then_inc(work_taken[b], 1)

            act.wait_ge(params_in, 16 * N_PARAMS)
            act.wait_ge(params_ready, 2)
            scale = float(HD) ** -0.5
            nc.scalar.activation(bqkv[:, 1:3], bank[0][:, 1:3], ACT.Copy).then_inc(params_ready, 1)
            nc.scalar.activation(bqkv[:, 0:1], bank[0][:, 0:1], ACT.Copy, scale=scale)\
              .then_inc(params_ready, 1)
            nc.scalar.activation(bf1[:, :], bank[0][:, 3:5], ACT.Copy).then_inc(params_ready, 1)
            for i in range(PIECES):
                square(i)
            for t, (kind, i) in enumerate(FIRST_TASKS):
                take(kind, i, t % 2, t // 2)

            def group(g, last):
                tasks = tasks_of(g, last)
                for s in range(SLOTS):
                    for ts, kind, i, b, fill in tasks:
                        if ts == s and kind not in ("YT", "PROJ"):
                            take(kind, i, b, fill)
                    if 1 <= s <= QUADS:
                        q = s - 1
                        act.wait_ge(shifted[q % 2], (QUADS // 2) * g + q // 2 + 1)
                        nc.scalar.activation(probs[q % 4][:, :], probs[q % 4][:, :], ACT.Exp)\
                          .then_inc(probs_ready, 1)
                    if TR_LAG <= s < QUADS + TR_LAG:
                        q = s - TR_LAG
                        b = q % 2
                        act.wait_ge(trans_ready[b], (QUADS // 2) * g + q // 2 + 1)
                        nc.scalar.activation(probsT[b][:, :], trans[b][:, :], ACT.Copy)\
                          .then_inc(trans_copied[b], 1)
                    if PV_LAG <= s < QUADS + PV_LAG:
                        b = (s - PV_LAG) % 2
                        act.wait_ge(outs_ready[b], (QUADS // 2) * g + (s - PV_LAG) // 2 + 1)
                        nc.scalar.activation(rT[b][:, :], outs[b][:, P:2 * P], ACT.Copy)\
                          .then_inc(rT_copied[b], 1)
                    for ts, kind, i, b, fill in tasks:
                        if ts == s and kind == "PROJ":
                            take(kind, i, b, fill)
                    if (i := ln_piece(s, 1, last)) is not None:
                        square(PIECES * (g + 1) + i)

            with act.Fori(0, GROUPS - 1) as g:
                group(g, False)
            group(GROUPS - 1, True)

            S = GROUPS * PIECES

            def step(s, par, hid, copy):
                if hid:
                    for j in range(4):
                        act.wait_ge(fc1_ready, 4 * s + j + 1)
                        nc.scalar.activation(hidden[par][:, j, :], bank[1 + j][:, :],
                                             ACT.Gelu_apprx_tanh, bias=bf1[:, j % 2:j % 2 + 1])\
                          .then_inc(gelu_done, 1)
                if copy:
                    act.wait_ge(fc2_ready, s)
                    nc.scalar.activation(y2T[1 - par][:, :], bank[5][:, :], ACT.Identity,
                                         bias=bf2[:, 0:1]).then_inc(y2T_copied, 1)

            square(S)
            for s in range(-1, 4):
                if s >= 0:
                    step(s, s % 2, True, s >= 1)
                square(S + s + 2)
            with act.Fori(2, (S - 4) // 2 + 1) as k:
                for d in range(2):
                    step(2 * k + d, d, True, True)
                    square(S + 2 * k + d + 2)
            for s in range(S - 2, S + 1):
                step(s, s % 2, s < S, True)

        @block.tensor
        def _(pe):
            def mm(out, lhsT, rhs, start=True, stop=True):
                return nc.tensor.matmul(out, lhsT, rhs, start=start, stop=stop)

            def fill(kind, i, b, before):
                if not isinstance(before, int) or before:
                    pe.wait_ge(work_taken[b], before)
                par, out = i % 2, work[b]
                if kind == "XT":
                    for k in range(4):
                        jj = 4 * i + k
                        done = nc.tensor.transpose(out[:, k * P:(k + 1) * P],
                                                   xn[:, jj * P:(jj + 1) * P], ident[:, :])
                elif kind in ("Q", "K", "V"):
                    done = mm(out[:, :], wqkv[:, "QKV".index(kind), :],
                              xT[:, i % GI * IMG:(i % GI + 1) * IMG])
                elif kind == "VT":
                    for k in range(4):
                        done = nc.tensor.transpose(out[:, k * P:(k + 1) * P],
                                                   vT[par][:, k * P:(k + 1) * P], ident[:, :])
                elif kind == "PROJ":
                    done = mm(out[:, :], wproj[:, :], oT[par][:, :])
                elif kind == "YT":
                    for k in range(4):
                        jj = 4 * i + k
                        done = nc.tensor.transpose(out[:, k * P:(k + 1) * P],
                                                   yT[:, jj * P:(jj + 1) * P], ident[:, :])
                done.then_inc(work_ready[b], 1)

            pe.wait_ge(params_in, 16 * N_PARAMS)
            pe.wait_ge(pool_ready, 2)
            for t in range(3):
                mm(bank[0][:, t:t + 1], wraw[:, t, :], shift[:, 0:1], stop=False)
                mm(bank[0][:, t:t + 1], ident[:, :], bqkv_raw[:, t:t + 1], start=False)
            for t in range(2):
                mm(bank[0][:, 3 + t:4 + t], w1raw[:, t, :], shift[:, 1:2], stop=False)
                done = mm(bank[0][:, 3 + t:4 + t], ident[:, :], bf1_raw[:, t:t + 1], start=False)
            done.then_inc(params_ready, 1)

            pe.wait_ge(xn_ready, PIECES)
            pe.wait_ge(params_ready, 5)
            for t, (kind, i) in enumerate(FIRST_TASKS):
                if kind == "K":
                    pe.wait_ge(work_taken[1], t // 2)
                if kind == "VT":
                    pe.wait_ge(work_taken[(t - 1) % 2], (t - 1) // 2 + 1)
                fill(kind, i, t % 2, t // 2)
            for b in range(2):
                pe.wait_ge(work_taken[b], FIRST_FILLS)
            pe.wait_ge(zeroed, 2)

            def group(g, last):
                tasks = tasks_of(g, last)
                place = {(kind, i): (b, before) for _, kind, i, b, before in tasks}

                def copied(kind, i):
                    b, before = place[kind, i]
                    pe.wait_ge(work_taken[b], before + 1)

                for s in range(SLOTS):
                    if s < QUADS:
                        image, wi = divmod(s, 4)
                        par, b, before = image % 2, s % 2, (QUADS // 2) * g + s // 2
                        if wi == 0:
                            pe.wait_ge(kX_loaded[par], 16 * KX_DMAS * (2 * g + image // 2 + 1))
                            if image:
                                copied("Q", image)
                        pe.wait_ge(scores_taken[b], before + 1)
                        for p in range(2):
                            at = wi * P + p * N
                            for w in range(2):
                                out = scores[b][w * N:(w + 1) * N, :]\
                                    .rearrange("q (h p m) -> q p h m", h=HEADS, p=2)[:, p]
                                done = mm(out, qT[par][:, at:at + N],
                                          kX[par][:, HEADS * w:HEADS * (w + 1), at:at + N])
                        done.then_inc(scores_ready[b], 1)
                    for ts, kind, i, b, before in tasks:
                        if ts != s or kind in ("YT", "PROJ"):
                            continue
                        if kind == "VT":
                            copied("V", i)
                        if kind == "K" and i == GI:
                            copied("XT", 2)
                            copied("XT", 3)
                        if kind == "XT" and i == 0:
                            pe.wait_ge(xn_ready, PIECES * (g + 2))
                        fill(kind, i, b, before)
                    if TR_LAG <= s < QUADS + TR_LAG:
                        q = s - TR_LAG
                        b = q % 2
                        pe.wait_ge(probs_ready, QUADS * g + q + 1)
                        for h in range(HEADS):
                            done = nc.tensor.transpose(trans[b][:, h * P:(h + 1) * P],
                                                       probs[q % 4][:, h * P:(h + 1) * P], ident[:, :])
                        done.then_inc(trans_ready[b], 1)
                    if PV_LAG <= s < QUADS + PV_LAG:
                        q = s - PV_LAG
                        image, wi = divmod(q, 4)
                        b, before = q % 2, (QUADS // 2) * g + q // 2
                        if wi == 0 and image:
                            copied("VT", image)
                        pe.wait_ge(trans_copied[b], before + 1)
                        pe.wait_ge(outs_taken[b], before + 1)
                        for w in range(2):
                            for h in range(HEADS):
                                mm(outs[b][2 * HD * h:2 * HD * (h + 1), w * N:(w + 1) * N],
                                   vX[image % 2][:, (wi * 2 + w) * HEADS + h, :],
                                   probsT[b][:, (2 * h + w) * N:(2 * h + w + 1) * N])
                        pe.wait_ge(recip_ready, QUADS * g + q + 1)
                        nc.tensor.transpose(outs[b][:, P:2 * P], recip[q % 4][:, :], ident[:, :])\
                          .then_inc(outs_ready[b], 1)
                    for ts, kind, i, b, before in tasks:
                        if ts != s or kind not in ("YT", "PROJ"):
                            continue
                        if kind == "PROJ":
                            pe.wait_ge(outs_taken[0], (QUADS // 2) * g + 2 * i + 3)
                            pe.wait_ge(outs_taken[1], (QUADS // 2) * g + 2 * i + 3)
                        elif i == 0:
                            copied("PROJ", GI - 1)
                        fill(kind, i, b, before)

            with pe.Fori(0, GROUPS - 1) as g:
                group(g, False)
            group(GROUPS - 1, True)

            S = GROUPS * PIECES
            for b in range(2):
                pe.wait_ge(scores_taken[b], S * 2 + 1)
                pe.wait_ge(trans_copied[b], S * 2)
                pe.wait_ge(outs_taken[b], S * 2 + 1)
                pe.wait_ge(work_taken[b], ALL_FILLS)

            def step(s, par, f1, xt, f2, y):
                if f1:
                    pe.wait_ge(xT2_copied, s + 1)
                    for j in range(4):
                        if not isinstance(s, int) or s:
                            pe.wait_ge(gelu_done, 4 * s + j - 3)
                        mm(bank[1 + j][:, :], w1[:, j, :], xT2[par][:, :]).then_inc(fc1_ready, 1)
                if xt:
                    pe.wait_ge(xn_ready, S + s + 2)
                    if not isinstance(s, int) or s >= 0:
                        pe.wait_ge(xT2_copied, s + 1)
                    for k in range(4):
                        at = (1 - par) * PIECE + k * P
                        done = nc.tensor.transpose(bank[0][:, k * P:(k + 1) * P], xn[:, at:at + P],
                                                   ident[:, :])
                    done.then_inc(xT2_ready, 1)
                if f2:
                    pe.wait_ge(gelu_done, 4 * s)
                    if not isinstance(s, int) or s >= 2:
                        pe.wait_ge(y2T_copied, s - 1)
                    for half in range(2):
                        for w in range(2):
                            done = mm(bank[5][C * w:C * (w + 1), :], w2[:, half, :],
                                      hidden[1 - par][:, 2 * w + half, :], start=half == 0,
                                      stop=half == 1)
                    done.then_inc(fc2_ready, 1)
                if y:
                    pe.wait_ge(y2T_copied, s - 1)
                    if not isinstance(s, int) or s >= 3:
                        pe.wait_ge(out_ready, s - 2)
                    for k in range(4):
                        done = nc.tensor.transpose(bank[6][:, k * P:(k + 1) * P],
                                                   y2T[par][:, k * P:(k + 1) * P], ident[:, :])
                    done.then_inc(y2_ready, 1)

            for s in range(-1, 4):
                step(s, s % 2, s >= 0, True, s >= 1, s >= 2)
            with pe.Fori(2, (S - 4) // 2 + 1) as k:
                for d in range(2):
                    step(2 * k + d, d, True, True, True, True)
            for s in range(S - 2, S + 2):
                step(s, s % 2, s < S, s + 1 < S, s <= S, True)


_PARAMS = ["ln1_g", "ln1_b", "qkv_w", "qkv_b", "proj_w", "proj_b", "rpb", "ln2_g", "ln2_b", "fc1_w",
           "fc1_b", "fc2_w", "fc2_b"]


def kernel(**inputs):
    import concourse.bacc as bacc
    from concourse.bass_utils import run_bass_kernel_spmd

    arrays = {"x": np.ascontiguousarray(inputs["x"])}
    for name in _PARAMS:
        arrays[name] = np.ascontiguousarray(inputs["L0_conv_" + name])
    arrays["rpb"] = np.ascontiguousarray(
        arrays["rpb"][rel_pos_index()].transpose(0, 2, 1).reshape(N, HEADS * N))
    arrays["mask"] = shift_masks()

    nc = bacc.Bacc("TRN2", target_bir_lowering=False, num_devices=1)
    args = [nc.dram_tensor(f"in_{name}", a.shape, mybir.dt.from_np(a.dtype), kind="ExternalInput").ap()
            for name, a in arrays.items()]
    out = nc.dram_tensor("out", arrays["x"].shape, F32, kind="ExternalOutput").ap()
    build(nc, *args, out)
    r = run_bass_kernel_spmd(nc, [{f"in_{name}": a for name, a in arrays.items()}], core_ids=[0])
    return r.results[0]["out"]
```

```python
from contextlib import ExitStack

import numpy as np

import concourse.bass as bass
from concourse import mybir

F32 = mybir.dt.float32
ACT = mybir.ActivationFunctionType
ALU = mybir.AluOpType
AXX = mybir.AxisListType.X

P = 128
BATCH, SIDE, C = 32, 32, 64
WIN, SHIFT, HEADS = 8, 4, 4
HD = C // HEADS
N = WIN * WIN
FF = 4 * C
GI = P // SIDE
GROUPS = BATCH // GI
ROW = SIDE * C
PIECE = WIN * C
PIECES = ROW // PIECE
QUADS = (SIDE // WIN) * GI
BANK = 512
IMG = 4 * P
EPS = 1e-5
NEG = -1e9


def rel_pos_index():
    at = np.stack(np.meshgrid(np.arange(WIN), np.arange(WIN), indexing="ij")).reshape(2, -1)
    rel = (at[:, :, None] - at[:, None, :]).transpose(1, 2, 0) + (WIN - 1)
    return rel[..., 0] * (2 * WIN - 1) + rel[..., 1]


def shift_masks():
    region = np.zeros((SIDE, SIDE), np.int32)
    parts = (slice(0, -WIN), slice(-WIN, -SHIFT), slice(-SHIFT, None))
    for a, hs in enumerate(parts):
        for b, ws in enumerate(parts):
            region[hs, ws] = 3 * a + b
    k = SIDE // WIN
    win = region.reshape(k, WIN, k, WIN).transpose(0, 2, 1, 3).reshape(k, k, N)
    out = np.zeros((2, N, 2, 2, N), np.float32)
    for v, wi in enumerate((0, k - 1)):
        for wj in range(k):
            differ = win[wi, wj][:, None] != win[wi, wj][None, :]
            out[wj % 2, :, v, wj // 2, :] = np.where(differ, NEG, 0.0)
    return out.reshape(P, 2 * P)


TR_LAG, PV_LAG = 2, 3
SLOTS = QUADS + 4
LN_SLOTS = {"sum": (2, 2, 3, 3), "centre": (4, 5, 6, 7), "square": (6, 7, 8, 8),
            "square_sum": (7, 8, 9, 9), "scale": (10, 11, 12, 13)}


def ln_pieces(stage, s, last):
    return [i for i, at in enumerate(LN_SLOTS[stage]) if at == s and not last]


def bank_tasks(last):
    tasks = []
    for s in range(SLOTS):
        image, r = divmod(s, 4)
        if s < QUADS - 4:
            tasks.append((s, ("K", "Q", "V", "VT")[r], image + 1))
        elif not last and QUADS - 4 < s < QUADS:
            tasks.append((s, "XT", s - (QUADS - 3)))
            if s == QUADS - 1:
                tasks.append((s, "XT", 3))
        elif not last and s == QUADS:
            tasks.append((s, "K", GI))
        elif not last and s == QUADS + 1:
            tasks += [(s, "Q", GI), (s, "V", GI)]
        elif not last and s == QUADS + 2:
            tasks.append((s, "VT", GI))
        if s >= 7 and s % 4 == 3:
            tasks.append((s, "PROJ", s // 4 - 1))
    tasks += [(SLOTS - 1, "YT", j) for j in range(4)]
    return tasks


FIRST_TASKS = [("XT", 0), ("XT", 1), ("XT", 2), ("XT", 3), ("K", 0), ("Q", 0), ("V", 0), ("VT", 0)]
FIRST_FILLS = len(FIRST_TASKS) // 2
GROUP_FILLS = len(bank_tasks(False)) // 2
LAST_FILLS = len(bank_tasks(True)) // 2
ALL_FILLS = FIRST_FILLS + (GROUPS - 1) * GROUP_FILLS + LAST_FILLS


PARAM_COLUMNS = [("wqkv", 3 * P), ("gain", 2), ("shift", 2), ("bqkv", 3), ("bf1", 2), ("bproj", 1),
                 ("bf2", 1), ("rpb", HEADS * N), ("mask", 2 * P), ("wproj", P), ("w1", 4 * P),
                 ("w2", 2 * C)]


def build(nc, x_d, params_d, out_d):
    with ExitStack() as ctx:
        def sb(name, *shape):
            return ctx.enter_context(nc.sbuf_tensor(name, [P, *shape], F32))

        def sem(name):
            return ctx.enter_context(nc.semaphore(name))

        bank = [ctx.enter_context(nc.psum_tensor(f"bank{i}", [P, BANK], F32)) for i in range(8)]

        x = sb("x", GROUPS * ROW)
        xn = sb("xn", ROW)
        xT = sb("xT", GI * IMG)
        yT = sb("yT", GI * IMG)
        qT = [sb(f"qT{i}", IMG) for i in range(2)]
        kT = [sb(f"kT{i}", IMG) for i in range(2)]
        vT = [sb(f"vT{i}", IMG) for i in range(2)]
        kX = [sb(f"kX{i}", 2 * HEADS, IMG) for i in range(2)]
        vX = [sb(f"vX{i}", 4 * 2 * HEADS, 2 * HD) for i in range(2)]
        probs = [sb(f"probs{i}", BANK) for i in range(4)]
        probsT = [sb(f"probsT{i}", BANK) for i in range(2)]
        oT = [sb(f"oT{i}", IMG) for i in range(2)]
        rT = [sb(f"rT{i}", P) for i in range(2)]
        recip = [sb(f"recip{i}", P) for i in range(4)]
        negmax = [sb(f"negmax{i}", 8) for i in range(4)]
        rowsum = [sb(f"rowsum{i}", 8) for i in range(4)]
        squares = [sb(f"squares{i}", PIECE) for i in range(2)]
        stat_sum = sb("stat_sum", SIDE)
        stat_mean = sb("stat_mean", SIDE)
        stat_sq = sb("stat_sq", SIDE)
        stat_var = sb("stat_var", SIDE)
        stat_rstd = sb("stat_rstd", SIDE)
        minus_half = sb("minus_half", SIDE)
        one_over_c = sb("one_over_c", SIDE)
        eps = sb("eps", SIDE)
        inverse = [sb(f"inverse{i}", 2 * HEADS) for i in range(4)]
        ident = sb("ident", P)
        bias = [sb(f"bias{i}", BANK) for i in range(2)]
        params = sb("params", sum(width for _, width in PARAM_COLUMNS))

        def param(name):
            at = 0
            for other, width in PARAM_COLUMNS:
                if other == name:
                    return params[:, at:at + width]
                at += width

        wraw = param("wqkv").rearrange("q (t o) -> q t o", t=3)
        w1raw = param("w1").rearrange("q (t o) -> q t o", t=4)
        w2 = param("w2").rearrange("q (t o) -> q t o", t=2)
        wproj, rpb, mask = param("wproj"), param("rpb"), param("mask")
        gain, shift, bqkv_raw, bf1_raw = (param(k) for k in ("gain", "shift", "bqkv", "bf1"))
        bproj, bf2 = param("bproj"), param("bf2")
        wqkv = sb("wqkv", 3, P)
        w1 = sb("w1", 4, P)
        bqkv = sb("bqkv", 3)
        bf1 = sb("bf1", 2)
        xT2 = [sb(f"xT2_{i}", BANK) for i in range(2)]
        hidden = [sb(f"hidden{i}", 4, BANK) for i in range(1)] + [kX[1][:, 0:4, :]]
        y2T = [sb(f"y2T{i}", BANK) for i in range(2)]

        scores = bank[0:2]
        trans = bank[2:4]
        outs = bank[4:6]
        work = bank[6:8]

        x_loaded, params_in = sem("x_loaded"), sem("params_in")
        pool_ready, zeroed = sem("pool_ready"), sem("zeroed")
        params_ready, bias_made = sem("params_ready"), sem("bias_made")
        scores_ready = [sem(f"scores_ready{i}") for i in range(2)]
        scores_taken = [sem(f"scores_taken{i}") for i in range(2)]
        negmax_ready = sem("negmax_ready")
        shifted = sem("shifted")
        probs_ready = sem("probs_ready")
        sum_ready, inverse_ready = sem("sum_ready"), sem("inverse_ready")
        recip_ready = sem("recip_ready")
        trans_ready = [sem(f"trans_ready{i}") for i in range(2)]
        trans_copied = [sem(f"trans_copied{i}") for i in range(2)]
        outs_ready = [sem(f"outs_ready{i}") for i in range(2)]
        rT_copied = [sem(f"rT_copied{i}") for i in range(2)]
        outs_taken = [sem(f"outs_taken{i}") for i in range(2)]
        work_ready = [sem(f"work_ready{i}") for i in range(2)]
        work_taken = [sem(f"work_taken{i}") for i in range(2)]
        kX_loaded = [sem(f"kX_loaded{i}") for i in range(2)]
        ln_sum, ln_mean, ln_centred = sem("ln_sum"), sem("ln_mean"), sem("ln_centred")
        ln_squares, ln_sq, ln_var = sem("ln_squares"), sem("ln_sq"), sem("ln_var")
        ln_eps, ln_rstd, xn_ready = sem("ln_eps"), sem("ln_rstd"), sem("xn_ready")
        xT2_ready, xT2_copied = sem("xT2_ready"), sem("xT2_copied")
        fc1_ready, gelu_done = sem("fc1_ready"), sem("gelu_done")
        fc2_ready, y2T_copied = sem("fc2_ready"), sem("y2T_copied")
        y2_ready, out_ready, stored = sem("y2_ready"), sem("out_ready"), sem("stored")

        COPIES = SIDE // WIN * 2
        KX_DMAS = 2 * HEADS

        S = GROUPS * PIECES

        block = ctx.enter_context(nc.Block())

        def group_base(g):
            return FIRST_FILLS + GROUP_FILLS * g

        def tasks_of(g, last):
            return [(s, kind, i, t % 2, group_base(g) + t // 2)
                    for t, (s, kind, i) in enumerate(bank_tasks(last))]

        def rows_of(group_dma, g):
            for a in range(GI):
                for r0, r1, s0 in ((0, SIDE - SHIFT, SHIFT), (SIDE - SHIFT, SIDE, 0)):
                    hbm = group_dma[bass.ds(g * GI + a, 1), s0:s0 + r1 - r0]
                    yield (x[SIDE * a + r0:SIDE * a + r1, bass.ds(g * ROW, ROW)],
                           hbm.rearrange("o r c f -> (o r) (c f)"))

        @block.sync
        def _(sp):
            def load(g):
                for dst, src in rows_of(x_d, g):
                    sp.dma_start(dst, src).then_inc(x_loaded, 16)

            def spread_keys(par, fill):
                for j in range(2 * HEADS):
                    rows = slice(HD * j, HD * (j + 1))
                    sp.dma_start(kX[par][rows, j, :], kT[par][rows, :]).then_inc(kX_loaded[par], 16)

            sp.dma_start(params[:, :], params_d).then_inc(params_in, 16)
            load(0)
            sp.wait_ge(zeroed, 2)
            sp.wait_ge(work_taken[0], 3)
            spread_keys(0, 0)

            def group(g, last):
                if not last:
                    sp.wait_ge(x_loaded, 16 * COPIES * (g + 1))
                    load(g + 1)
                for s, kind, i, b, fill in tasks_of(g, last):
                    if kind == "K":
                        sp.wait_ge(work_taken[b], fill + 1)
                        spread_keys(i % 2, g)

            with sp.Fori(0, GROUPS - 1) as g:
                group(g, False)
            group(GROUPS - 1, True)

            with sp.Fori(0, GROUPS) as g:
                sp.wait_ge(out_ready, PIECES * g + PIECES)
                for src, dst in rows_of(out_d, g):
                    sp.dma_start(dst, src).then_inc(stored, 16)
            sp.wait_ge(stored, 16 * COPIES * GROUPS)

        @block.gpsimd
        def _(pool):
            nc.gpsimd.memset(minus_half[:, :], -0.5)
            nc.gpsimd.memset(one_over_c[:, :], 1.0 / C)
            nc.gpsimd.memset(eps[:, :], EPS)
            nc.gpsimd.memset(ident[:, :], 0.0).then_inc(pool_ready, 1)
            pool.wait_ge(pool_ready, 1)
            nc.gpsimd.affine_select(out=ident[:, :], in_=ident[:, :], compare_op=ALU.not_equal,
                                    fill=1.0, base=0, pattern=[[-1, P]], channel_multiplier=1)\
              .then_inc(pool_ready, 1)
            nc.gpsimd.memset(kX[1][:, :, :], 0.0).then_inc(zeroed, 1)

            def mean(n, u, cols):
                pool.wait_ge(ln_sum, u)
                nc.gpsimd.tensor_tensor(stat_mean[:, cols], stat_sum[:, cols], one_over_c[:, cols],
                                        ALU.mult).then_inc(ln_mean, 1)
                pool.wait_ge(ln_mean, n + 1)

            def rstd(n, u, cols):
                pool.wait_ge(ln_sq, u)
                nc.gpsimd.tensor_tensor(stat_var[:, cols], stat_sq[:, cols], eps[:, cols], ALU.add)\
                  .then_inc(ln_var, 1)
                pool.wait_ge(ln_var, n + 1)
                nc.gpsimd.tensor_tensor(stat_rstd[:, cols], stat_var[:, cols], minus_half[:, cols],
                                        ALU.pow).then_inc(ln_rstd, 1)
                pool.wait_ge(ln_rstd, n + 1)

            def centre(dst, src, c0, n):
                m = stat_mean[:, c0:c0 + n].unsqueeze(2).to_broadcast([P, n, C])
                return nc.gpsimd.tensor_tensor(dst, src.rearrange("q (a f) -> q a f", f=C), m, ALU.add)

            def scale(j):
                chunk = xn[:, j * PIECE:(j + 1) * PIECE].rearrange("q (a f) -> q a f", f=C)
                r = stat_rstd[:, j * WIN:(j + 1) * WIN].unsqueeze(2).to_broadcast([P, WIN, C])
                nc.gpsimd.tensor_tensor(chunk, chunk, r, ALU.mult).then_inc(xn_ready, 1)

            xn_v = xn[:, :].rearrange("q (p c w f) -> q p c w f", p=2, c=WIN, w=2)

            def centre_piece(G, i):
                before = (i - 1) % PIECES
                at = G * ROW + i * PIECE
                half = SHIFT * C
                centre(xn_v[:, before // 2, SHIFT:WIN, before % 2, :], x[:, bass.ds(at, half)],
                       i * WIN, SHIFT)
                centre(xn_v[:, i // 2, 0:SHIFT, i % 2, :], x[:, bass.ds(at + half, half)],
                       i * WIN + SHIFT, SHIFT).then_inc(ln_centred, 1)

            every = slice(0, SIDE)
            mean(0, PIECES, every)
            for i in range(PIECES):
                centre_piece(0, i)
            rstd(0, PIECES, every)

            def group(g, last):
                for s in range(QUADS):
                    pool.wait_ge(negmax_ready, QUADS * g + s + 1)
                    top = negmax[s % 4][:, :].unsqueeze(2).to_broadcast([P, 8, N])
                    e = probs[s % 4][:, :].rearrange("q (a m) -> q a m", m=N)
                    nc.gpsimd.tensor_tensor(e, e, top, ALU.add).then_inc(shifted, 1)
                    for i in ln_pieces("centre", s, last):
                        if i == 0:
                            mean(g + 1, PIECES * (g + 2), every)
                        centre_piece(g + 1, i)
                    for j in ln_pieces("scale", s, last):
                        if j == 0:
                            rstd(g + 1, PIECES * (g + 2), every)
                        scale(j)

            with pool.Fori(0, GROUPS - 1) as g:
                group(g, False)
            group(GROUPS - 1, True)

            def centre2(s, r):
                cols = slice(r * WIN, (r + 1) * WIN)
                mean(GROUPS + s, S + s + 1, cols)
                if not isinstance(s, int) or s >= 4:
                    pool.wait_ge(xT2_ready, s - 3)
                centre(xn[:, r * PIECE:(r + 1) * PIECE].rearrange("q (a f) -> q a f", f=C),
                       x[:, bass.ds(s * PIECE, PIECE)], r * WIN, WIN).then_inc(ln_centred, 1)

            def scale2(s, r):
                rstd(GROUPS + s, S + s + 1, slice(r * WIN, (r + 1) * WIN))
                scale(r)

            for s in range(3):
                centre2(s, s)
            scale2(0, 0)
            for s in range(-1, 4):
                scale2(s + 2, (s + 2) % 4)
                centre2(s + 4, (s + 4) % 4)
            with pool.Fori(1, S // 4 - 1) as k:
                for d in range(4):
                    scale2(4 * k + d + 2, (d + 2) % 4)
                    centre2(4 * k + d + 4, d)
            for s in range(S - 4, S - 2):
                scale2(s + 2, (s + 2) % 4)

        @block.vector
        def _(dve):
            def row_sum(src, cols, n, u):
                if not isinstance(n, int) or n:
                    dve.wait_ge(ln_mean, n)
                nc.vector.tensor_reduce(stat_sum[:, cols], src.rearrange("q (a f) -> q a f", f=C), AXX,
                                        ALU.add, negate=True).then_inc(ln_sum, 1)

            def square_sum(j, r, u):
                dve.wait_ge(ln_squares, u + 1)
                nc.vector.tensor_reduce(stat_sq[:, r * WIN:(r + 1) * WIN],
                                        squares[j % 2][:, :].rearrange("q (a f) -> q a f", f=C),
                                        AXX, ALU.add).then_inc(ln_sq, 1)

            nc.vector.memset(kX[0][:, :, :], 0.0)
            nc.vector.memset(vX[0][:, :, :], 0.0)
            nc.vector.memset(vX[1][:, :, :], 0.0).then_inc(zeroed, 1)
            for b in range(2):
                dve.sem_inc(scores_taken[b], 1)
                dve.sem_inc(outs_taken[b], 1)
            dve.wait_ge(x_loaded, 16 * COPIES)
            for i in range(PIECES):
                row_sum(x[:, i * PIECE:(i + 1) * PIECE], slice(i * WIN, (i + 1) * WIN), 0, i)
            dve.wait_ge(params_in, 16)
            for t in range(3):
                nc.vector.tensor_scalar(wqkv[:, t, :], wraw[:, t, :], gain[:, 0:1], None, ALU.mult)
            for t in range(4):
                last = nc.vector.tensor_scalar(w1[:, t, :], w1raw[:, t, :], gain[:, 1:2], None,
                                               ALU.mult)
            last.then_inc(params_ready, 1)
            for v in range(2):
                r = rpb[:, :].rearrange("q (h m) -> q h m", h=HEADS).unsqueeze(2)\
                    .to_broadcast([P, HEADS, 2, N])
                m = mask[:, v * P:(v + 1) * P].rearrange("q (p m) -> q p m", p=2).unsqueeze(1)\
                    .to_broadcast([P, HEADS, 2, N])
                nc.vector.tensor_tensor(bias[v][:, :].rearrange("q (h p m) -> q h p m", h=HEADS, p=2),
                                        r, m, ALU.add).then_inc(bias_made, 1)
            for j in range(PIECES):
                square_sum(j, j, j)
            dve.wait_ge(ln_rstd, 1)
            for j in range(PIECES):
                chunk = xn[:, j * PIECE:(j + 1) * PIECE].rearrange("q (a f) -> q a f", f=C)
                r = stat_rstd[:, j * WIN:(j + 1) * WIN].unsqueeze(2).to_broadcast([P, WIN, C])
                nc.vector.tensor_tensor(chunk, chunk, r, ALU.mult).then_inc(xn_ready, 1)
            dve.wait_ge(bias_made, 2)

            def group(g, last):
                tasks = tasks_of(g, last)
                for s in range(SLOTS):
                    if s < QUADS:
                        b, fill = s % 2, (QUADS // 2) * g + s // 2
                        e = probs[s % 4]
                        dve.wait_ge(scores_ready[b], fill + 1)
                        nc.vector.tensor_tensor(e[:, :], scores[b][:, :],
                                                bias[s % 4 == 3][:, :], ALU.add)\
                          .then_inc(scores_taken[b], 1)
                        dve.wait_ge(scores_taken[b], fill + 2)
                        e3 = e[:, :].rearrange("q (a m) -> q a m", m=N)
                        nc.vector.tensor_reduce(negmax[s % 4][:, :], e3, AXX, ALU.max, negate=True)\
                          .then_inc(negmax_ready, 1)
                    if 1 <= s < QUADS + 1:
                        q = s - 1
                        dve.wait_ge(probs_ready, QUADS * g + q + 1)
                        nc.vector.tensor_reduce(rowsum[q % 4][:, :],
                                                probs[q % 4][:, :].rearrange("q (a m) -> q a m", m=N),
                                                AXX, ALU.add).then_inc(sum_ready, 1)
                    if s >= PV_LAG and s - PV_LAG < QUADS:
                        q = s - PV_LAG
                        b, fill = q % 2, (QUADS // 2) * g + q // 2
                        dve.wait_ge(rT_copied[b], fill + 1)
                        nc.vector.tensor_tensor(oT[q // 4 % 2][:, q % 4 * P:(q % 4 + 1) * P],
                                                outs[b][:, 0:P], rT[b][:, :], ALU.mult)\
                          .then_inc(outs_taken[b], 1)
                    if 1 <= s < QUADS + 1:
                        q = s - 1
                        dve.wait_ge(sum_ready, QUADS * g + q + 1)
                        nc.vector.reciprocal(inverse[q % 4][:, :], rowsum[q % 4][:, :])\
                          .then_inc(inverse_ready, 1)
                    for i in ln_pieces("sum", s, last):
                        if i == 0:
                            dve.wait_ge(x_loaded, 16 * COPIES * (g + 2))
                        row_sum(x[:, bass.ds((g + 1) * ROW + i * PIECE, PIECE)],
                                slice(i * WIN, (i + 1) * WIN), g + 1, PIECES * (g + 1) + i)
                    for j in ln_pieces("square_sum", s, last):
                        square_sum(j, j, PIECES * (g + 1) + j)
                    for ts, kind, j, b, fill in tasks:
                        if ts != s or kind != "YT":
                            continue
                        dve.wait_ge(work_ready[b], fill + 1)
                        w, c0 = j // 2, (j % 2) * SHIFT
                        src = work[b][:, :].rearrange("q (c p f) -> q c p f", c=4, p=2)
                        if (w, c0) != (1, SHIFT):
                            col = WIN * w + c0 + SHIFT
                            dst = x[:, bass.ds(g * ROW, ROW)]\
                                .rearrange("q (p c f) -> q c p f", p=2, f=C)[:, col:col + SHIFT]
                            nc.vector.tensor_tensor(dst, src, dst, ALU.add)\
                              .then_inc(work_taken[b], 1)
                            continue
                        for p, col in ((0, 2 * WIN), (1, 0)):
                            dst = x[:, bass.ds(g * ROW + col * C, SHIFT * C)]\
                                .rearrange("q (c f) -> q c f", f=C)
                            done = nc.vector.tensor_tensor(dst, src[:, :, p, :], dst, ALU.add)
                        done.then_inc(work_taken[b], 1)

            with dve.Fori(0, GROUPS - 1) as g:
                group(g, False)
            group(GROUPS - 1, True)
            for b in range(2):
                dve.wait_ge(work_taken[b], ALL_FILLS)

            def step(s, x_in, copy, add):
                if copy:
                    dve.wait_ge(xT2_ready, s + 2)
                    nc.vector.tensor_copy(xT2[(s + 1) % 2 if isinstance(s, int) else x_in][:, :],
                                          bank[0][:, :]).then_inc(xT2_copied, 1)
                if add:
                    dve.wait_ge(y2_ready, s - 1)
                    dst = x[:, bass.ds((s - 2) * PIECE, PIECE)]
                    nc.vector.tensor_tensor(dst, bank[6][:, :], dst, ALU.add).then_inc(out_ready, 1)

            def sum2(s, r):
                row_sum(x[:, bass.ds(s * PIECE, PIECE)], slice(r * WIN, (r + 1) * WIN),
                        GROUPS + (s - 3 if not isinstance(s, int) or s > 3 else 0), S + s)

            for s in range(3):
                sum2(s, s)
            for s in range(2):
                square_sum(s, s, S + s)
            for s in range(-1, 4):
                step(s, 0, True, s >= 2)
                sum2(s + 4, (s + 4) % 4)
                square_sum(s + 3, (s + 3) % 4, S + s + 3)
            with dve.Fori(1, S // 4 - 1) as k:
                for d in range(4):
                    step(4 * k + d, (d + 1) % 2, True, True)
                    sum2(4 * k + d + 4, d)
                    square_sum(d + 3, (d + 3) % 4, S + 4 * k + d + 3)
            for s in range(S - 4, S + 2):
                step(s, 0, s + 1 < S, True)
                if s + 3 < S:
                    square_sum(s + 3, (s + 3) % 4, S + s + 3)

        @block.scalar
        def _(act):
            def square(j, r, u, centred_u):
                act.wait_ge(ln_centred, centred_u)
                if not isinstance(u, int) or u >= 2:
                    act.wait_ge(ln_sq, u - 1)
                nc.scalar.activation(squares[j % 2][:, :], xn[:, r * PIECE:(r + 1) * PIECE], ACT.Square,
                                     scale=float(C) ** -0.5).then_inc(ln_squares, 1)

            def take(kind, i, b, fill):
                act.wait_ge(work_ready[b], fill + 1)
                src, par = work[b], i % 2
                if kind == "XT":
                    p, c0 = i // 2, i % 2 * 4
                    dst = xT[:, :].rearrange("q (i p r c) -> q p c i r", p=2, r=WIN, c=WIN)
                    done = nc.scalar.activation(
                        dst[:, p, c0:c0 + 4],
                        src[:, :].rearrange("q (c i r) -> q c i r", c=4, r=WIN), ACT.Copy)
                elif kind == "Q":
                    done = nc.scalar.activation(qT[par][:, :], src[:, :], ACT.Identity,
                                                bias=bqkv[:, 0:1], scale=float(HD) ** -0.5)
                elif kind == "K":
                    done = nc.scalar.activation(kT[par][:, :], src[:, :], ACT.Identity,
                                                bias=bqkv[:, 1:2])
                elif kind == "V":
                    done = nc.scalar.activation(vT[par][:, :], src[:, :], ACT.Identity,
                                                bias=bqkv[:, 2:3])
                elif kind == "VT":
                    for p in range(2):
                        half = slice(N * p, N * (p + 1))
                        done = nc.scalar.activation(
                            vX[par][half, :, HD * p:HD * (p + 1)],
                            src[half, :].rearrange("q (a d) -> q a d", d=HD), ACT.Copy)
                elif kind == "PROJ":
                    for w in range(2):
                        dst = yT[:, :].rearrange("q (w c i y r) -> q w i y r c", w=2, c=WIN, i=GI,
                                                 y=SIDE // WIN)
                        done = nc.scalar.activation(
                            dst[:, w, i],
                            src[:, :].rearrange("q (y w r c) -> q w y r c", y=SIDE // WIN, w=2,
                                                r=WIN)[:, w],
                            ACT.Identity, bias=bproj[:, 0:1])
                done.then_inc(work_taken[b], 1)

            act.wait_ge(params_in, 16)
            act.wait_ge(params_ready, 2)
            scale = float(HD) ** -0.5
            nc.scalar.activation(bqkv[:, 1:3], bank[0][:, 1:3], ACT.Copy).then_inc(params_ready, 1)
            nc.scalar.activation(bqkv[:, 0:1], bank[0][:, 0:1], ACT.Copy, scale=scale)\
              .then_inc(params_ready, 1)
            nc.scalar.activation(bf1[:, :], bank[0][:, 3:5], ACT.Copy).then_inc(params_ready, 1)
            for j in range(PIECES):
                square(j, j, j, PIECES if j == 3 else j + 2)
            for t, (kind, i) in enumerate(FIRST_TASKS):
                take(kind, i, t % 2, t // 2)

            def group(g, last):
                tasks = tasks_of(g, last)
                for s in range(SLOTS):
                    for ts, kind, i, b, fill in tasks:
                        if ts == s and kind not in ("YT", "PROJ"):
                            take(kind, i, b, fill)
                    if 1 <= s <= QUADS:
                        q = s - 1
                        act.wait_ge(shifted, QUADS * g + q + 1)
                        nc.scalar.activation(probs[q % 4][:, :], probs[q % 4][:, :], ACT.Exp)\
                          .then_inc(probs_ready, 1)
                    if TR_LAG <= s < QUADS + TR_LAG:
                        q = s - TR_LAG
                        b = q % 2
                        act.wait_ge(trans_ready[b], (QUADS // 2) * g + q // 2 + 1)
                        nc.scalar.activation(probsT[b][:, :], trans[b][:, :], ACT.Copy)\
                          .then_inc(trans_copied[b], 1)
                        act.wait_ge(inverse_ready, QUADS * g + q + 1)
                        nc.scalar.activation(recip[q % 4][:, :].rearrange("q (a d) -> q a d", d=HD),
                                             inverse[q % 4][:, :].unsqueeze(2)
                                             .to_broadcast([P, 2 * HEADS, HD]), ACT.Copy)\
                          .then_inc(recip_ready, 1)
                    if PV_LAG <= s < QUADS + PV_LAG:
                        b = (s - PV_LAG) % 2
                        act.wait_ge(outs_ready[b], (QUADS // 2) * g + (s - PV_LAG) // 2 + 1)
                        nc.scalar.activation(rT[b][:, :], outs[b][:, P:2 * P], ACT.Copy)\
                          .then_inc(rT_copied[b], 1)
                    for ts, kind, i, b, fill in tasks:
                        if ts == s and kind == "PROJ":
                            take(kind, i, b, fill)
                    for j in ln_pieces("square", s, last):
                        square(j, j, PIECES * (g + 1) + j,
                               PIECES * (g + 1) + (PIECES if j == 3 else j + 2))

            with act.Fori(0, GROUPS - 1) as g:
                group(g, False)
            group(GROUPS - 1, True)


            def step(s, par, hid, copy):
                if hid:
                    for j in range(4):
                        act.wait_ge(fc1_ready, 4 * s + j + 1)
                        nc.scalar.activation(hidden[par][:, j, :], bank[1 + j][:, :],
                                             ACT.Gelu_apprx_tanh, bias=bf1[:, j % 2:j % 2 + 1])\
                          .then_inc(gelu_done, 1)
                if copy:
                    act.wait_ge(fc2_ready, s)
                    nc.scalar.activation(y2T[1 - par][:, :], bank[5][:, :], ACT.Identity,
                                         bias=bf2[:, 0:1]).then_inc(y2T_copied, 1)

            def square2(s, r):
                square(r, r, S + s, S + s + 1)

            for s in range(2):
                square2(s, s)
            for s in range(-1, 4):
                square2(s + 3, (s + 3) % 4)
                if s >= 0:
                    step(s, s % 2, True, s >= 1)
            with act.Fori(1, S // 4 - 1) as k:
                for d in range(4):
                    square2(4 * k + d + 3, (d + 3) % 4)
                    step(4 * k + d, d % 2, True, True)
            for s in range(S - 4, S + 1):
                if s + 3 < S:
                    square2(s + 3, (s + 3) % 4)
                step(s, s % 2, s < S, True)

        @block.tensor
        def _(pe):
            def mm(out, lhsT, rhs, start=True, stop=True):
                return nc.tensor.matmul(out, lhsT, rhs, start=start, stop=stop)

            def fill(kind, i, b, before):
                if not isinstance(before, int) or before:
                    pe.wait_ge(work_taken[b], before)
                par, out = i % 2, work[b]
                if kind == "XT":
                    for k in range(4):
                        jj = 4 * i + k
                        done = nc.tensor.transpose(out[:, k * P:(k + 1) * P],
                                                   xn[:, jj * P:(jj + 1) * P], ident[:, :])
                elif kind in ("Q", "K", "V"):
                    done = mm(out[:, :], wqkv[:, "QKV".index(kind), :],
                              xT[:, i % GI * IMG:(i % GI + 1) * IMG])
                elif kind == "VT":
                    for k in range(4):
                        done = nc.tensor.transpose(out[:, k * P:(k + 1) * P],
                                                   vT[par][:, k * P:(k + 1) * P], ident[:, :])
                elif kind == "PROJ":
                    done = mm(out[:, :], wproj[:, :], oT[par][:, :])
                elif kind == "YT":
                    for k in range(4):
                        jj = 4 * i + k
                        done = nc.tensor.transpose(out[:, k * P:(k + 1) * P],
                                                   yT[:, jj * P:(jj + 1) * P], ident[:, :])
                done.then_inc(work_ready[b], 1)

            pe.wait_ge(params_in, 16)
            pe.wait_ge(pool_ready, 2)
            for t in range(3):
                mm(bank[0][:, t:t + 1], wraw[:, t, :], shift[:, 0:1], stop=False)
                mm(bank[0][:, t:t + 1], ident[:, :], bqkv_raw[:, t:t + 1], start=False)
            for t in range(2):
                mm(bank[0][:, 3 + t:4 + t], w1raw[:, t, :], shift[:, 1:2], stop=False)
                done = mm(bank[0][:, 3 + t:4 + t], ident[:, :], bf1_raw[:, t:t + 1], start=False)
            done.then_inc(params_ready, 1)

            pe.wait_ge(xn_ready, PIECES)
            pe.wait_ge(params_ready, 5)
            for t, (kind, i) in enumerate(FIRST_TASKS):
                if kind == "K":
                    pe.wait_ge(work_taken[1], t // 2)
                if kind == "VT":
                    pe.wait_ge(work_taken[(t - 1) % 2], (t - 1) // 2 + 1)
                fill(kind, i, t % 2, t // 2)
            for b in range(2):
                pe.wait_ge(work_taken[b], FIRST_FILLS)
            pe.wait_ge(zeroed, 2)

            def group(g, last):
                tasks = tasks_of(g, last)
                place = {(kind, i): (b, before) for _, kind, i, b, before in tasks}

                def copied(kind, i):
                    b, before = place[kind, i]
                    pe.wait_ge(work_taken[b], before + 1)

                for s in range(SLOTS):
                    if s < QUADS:
                        image, wi = divmod(s, 4)
                        par, b, before = image % 2, s % 2, (QUADS // 2) * g + s // 2
                        if wi == 0:
                            pe.wait_ge(kX_loaded[par], 16 * KX_DMAS * (2 * g + image // 2 + 1))
                            if image:
                                copied("Q", image)
                        pe.wait_ge(scores_taken[b], before + 1)
                        for p in range(2):
                            at = wi * P + p * N
                            for w in range(2):
                                out = scores[b][w * N:(w + 1) * N, :]\
                                    .rearrange("q (h p m) -> q p h m", h=HEADS, p=2)[:, p]
                                done = mm(out, qT[par][:, at:at + N],
                                          kX[par][:, HEADS * w:HEADS * (w + 1), at:at + N])
                        done.then_inc(scores_ready[b], 1)
                    for ts, kind, i, b, before in tasks:
                        if ts != s or kind in ("YT", "PROJ"):
                            continue
                        if kind == "VT":
                            copied("V", i)
                        if kind == "K" and i == GI:
                            copied("XT", 2)
                            copied("XT", 3)
                        if kind == "XT":
                            pe.wait_ge(xn_ready, PIECES * (g + 1) + i + 1)
                        fill(kind, i, b, before)
                    if TR_LAG <= s < QUADS + TR_LAG:
                        q = s - TR_LAG
                        b = q % 2
                        pe.wait_ge(probs_ready, QUADS * g + q + 1)
                        for h in range(HEADS):
                            done = nc.tensor.transpose(trans[b][:, h * P:(h + 1) * P],
                                                       probs[q % 4][:, h * P:(h + 1) * P], ident[:, :])
                        done.then_inc(trans_ready[b], 1)
                    if PV_LAG <= s < QUADS + PV_LAG:
                        q = s - PV_LAG
                        image, wi = divmod(q, 4)
                        b, before = q % 2, (QUADS // 2) * g + q // 2
                        if wi == 0 and image:
                            copied("VT", image)
                        pe.wait_ge(trans_copied[b], before + 1)
                        pe.wait_ge(outs_taken[b], before + 1)
                        for w in range(2):
                            for h in range(HEADS):
                                mm(outs[b][2 * HD * h:2 * HD * (h + 1), w * N:(w + 1) * N],
                                   vX[image % 2][:, (wi * 2 + w) * HEADS + h, :],
                                   probsT[b][:, (2 * h + w) * N:(2 * h + w + 1) * N])
                        pe.wait_ge(recip_ready, QUADS * g + q + 1)
                        nc.tensor.transpose(outs[b][:, P:2 * P], recip[q % 4][:, :], ident[:, :])\
                          .then_inc(outs_ready[b], 1)
                    for ts, kind, i, b, before in tasks:
                        if ts != s or kind not in ("YT", "PROJ"):
                            continue
                        if kind == "PROJ":
                            pe.wait_ge(outs_taken[0], (QUADS // 2) * g + 2 * i + 3)
                            pe.wait_ge(outs_taken[1], (QUADS // 2) * g + 2 * i + 3)
                        elif i == 0:
                            copied("PROJ", GI - 1)
                        fill(kind, i, b, before)

            with pe.Fori(0, GROUPS - 1) as g:
                group(g, False)
            group(GROUPS - 1, True)

            for b in range(2):
                pe.wait_ge(scores_taken[b], S * 2 + 1)
                pe.wait_ge(trans_copied[b], S * 2)
                pe.wait_ge(outs_taken[b], S * 2 + 1)
                pe.wait_ge(work_taken[b], ALL_FILLS)

            def step(s, par, chunk, f1, xt, f2, y):
                if f1:
                    pe.wait_ge(xT2_copied, s + 1)
                    for j in range(4):
                        if not isinstance(s, int) or s:
                            pe.wait_ge(gelu_done, 4 * s + j - 3)
                        mm(bank[1 + j][:, :], w1[:, j, :], xT2[par][:, :]).then_inc(fc1_ready, 1)
                if xt:
                    pe.wait_ge(xn_ready, S + s + 2)
                    if not isinstance(s, int) or s >= 0:
                        pe.wait_ge(xT2_copied, s + 1)
                    for k in range(4):
                        at = chunk * PIECE + k * P
                        done = nc.tensor.transpose(bank[0][:, k * P:(k + 1) * P], xn[:, at:at + P],
                                                   ident[:, :])
                    done.then_inc(xT2_ready, 1)
                if f2:
                    pe.wait_ge(gelu_done, 4 * s)
                    if not isinstance(s, int) or s >= 2:
                        pe.wait_ge(y2T_copied, s - 1)
                    for half in range(2):
                        for w in range(2):
                            done = mm(bank[5][C * w:C * (w + 1), :], w2[:, half, :],
                                      hidden[1 - par][:, 2 * w + half, :], start=half == 0,
                                      stop=half == 1)
                    done.then_inc(fc2_ready, 1)
                if y:
                    pe.wait_ge(y2T_copied, s - 1)
                    if not isinstance(s, int) or s >= 3:
                        pe.wait_ge(out_ready, s - 2)
                    for k in range(4):
                        done = nc.tensor.transpose(bank[6][:, k * P:(k + 1) * P],
                                                   y2T[par][:, k * P:(k + 1) * P], ident[:, :])
                    done.then_inc(y2_ready, 1)

            for s in range(-1, 4):
                step(s, s % 2, (s + 1) % 4, s >= 0, True, s >= 1, s >= 2)
            with pe.Fori(1, S // 4 - 1) as k:
                for d in range(4):
                    step(4 * k + d, d % 2, (d + 1) % 4, True, True, True, True)
            for s in range(S - 4, S + 2):
                step(s, s % 2, (s + 1) % 4, s < S, s + 1 < S, s <= S, True)


def pack_params(ln1_g, ln1_b, qkv_w, qkv_b, proj_w, proj_b, rpb, ln2_g, ln2_b, fc1_w, fc1_b, fc2_w,
                fc2_b):
    def twice(a):
        return np.concatenate([a, a])

    wqkv = np.zeros((2, C, 3, 2, C), np.float32)
    w1 = np.zeros((2, C, 2, 2, P), np.float32)
    wproj = np.zeros((HEADS, 2, HD, 2, C), np.float32)
    for k in range(2):
        wqkv[k, :, :, k] = qkv_w.reshape(C, 3, C)
        w1[k, :, k] = fc1_w.reshape(C, 2, P)
        wproj[:, k, :, k] = proj_w.reshape(HEADS, HD, C)
    columns = {
        "wqkv": wqkv.reshape(P, 3 * P), "w1": w1.reshape(P, 4 * P), "wproj": wproj.reshape(P, P),
        "w2": fc2_w.reshape(2, P, C).transpose(1, 0, 2).reshape(P, 2 * C),
        "gain": twice(np.stack([ln1_g, ln2_g], 1)), "shift": twice(np.stack([ln1_b, ln2_b], 1)),
        "bqkv": twice(qkv_b.reshape(3, C).T), "bf1": fc1_b.reshape(2, P).T,
        "bproj": twice(proj_b[:, None]), "bf2": twice(fc2_b[:, None]),
        "rpb": twice(rpb[rel_pos_index()].transpose(0, 2, 1).reshape(N, HEADS * N)),
        "mask": shift_masks(),
    }
    return np.ascontiguousarray(np.concatenate([columns[name] for name, _ in PARAM_COLUMNS], 1))


def kernel(**inputs):
    import concourse.bacc as bacc
    from concourse.bass_utils import run_bass_kernel_spmd

    x = np.ascontiguousarray(inputs["x"])
    params = pack_params(**{name.removeprefix("L0_conv_"): np.asarray(a)
                            for name, a in inputs.items() if name != "x"})
    nc = bacc.Bacc("TRN2", target_bir_lowering=False, num_devices=1)
    x_d = nc.dram_tensor("in_x", x.shape, F32, kind="ExternalInput").ap()
    params_d = nc.dram_tensor("in_params", params.shape, F32, kind="ExternalInput").ap()
    out_d = nc.dram_tensor("out", x.shape, F32, kind="ExternalOutput").ap()
    build(nc, x_d, params_d, out_d)
    r = run_bass_kernel_spmd(nc, [{"in_x": x, "in_params": params}], core_ids=[0])
    return r.results[0]["out"]
```

```python
from contextlib import ExitStack

import numpy as np

import concourse.bass as bass
from concourse import mybir

F32, F32R, I32 = mybir.dt.float32, mybir.dt.float32r, mybir.dt.int32
ACT = mybir.ActivationFunctionType
ALU = mybir.AluOpType
AXX = mybir.AxisListType.X

P = 128
BATCH, SIDE, C = 32, 32, 64
WIN, SHIFT, HEADS = 8, 4, 4
HD = C // HEADS
N = WIN * WIN
FF = 4 * C
GI = P // SIDE
GROUPS = BATCH // GI
ROW = SIDE * C
PIECE = WIN * C
PIECES = ROW // PIECE
QUADS = (SIDE // WIN) * GI
BANK = 512
IMG = 4 * P
EPS = 1e-5
NEG = -1e9
UPPER = -(1 << 12)


def rel_pos_index():
    at = np.stack(np.meshgrid(np.arange(WIN), np.arange(WIN), indexing="ij")).reshape(2, -1)
    rel = (at[:, :, None] - at[:, None, :]).transpose(1, 2, 0) + (WIN - 1)
    return rel[..., 0] * (2 * WIN - 1) + rel[..., 1]


def shift_masks():
    region = np.zeros((SIDE, SIDE), np.int32)
    parts = (slice(0, -WIN), slice(-WIN, -SHIFT), slice(-SHIFT, None))
    for a, hs in enumerate(parts):
        for b, ws in enumerate(parts):
            region[hs, ws] = 3 * a + b
    k = SIDE // WIN
    win = region.reshape(k, WIN, k, WIN).transpose(0, 2, 1, 3).reshape(k, k, N)
    out = np.zeros((2, N, 2, 2, N), np.float32)
    for v, wi in enumerate((0, k - 1)):
        for wj in range(k):
            differ = win[wi, wj][:, None] != win[wi, wj][None, :]
            out[wj % 2, :, v, wj // 2, :] = np.where(differ, NEG, 0.0)
    return out.reshape(P, 2 * P)


TR_LAG, PV_LAG, TAIL = 2, 3, 4
LN_SLOTS = {"sum": (0, 0, 1, 1), "centre": (1, 2, 3, 4), "square": (3, 4, 5, 6),
            "square_sum": (4, 5, 6, 7), "rstd": (5, 6, 7, 8), "scale": (9, 9, 10, 11)}


def ln_pieces(stage, s):
    return [i for i, at in enumerate(LN_SLOTS[stage]) if at == s]


def group_slots(last):
    return range(QUADS + TAIL if last else QUADS)


def at_lag(g, s, lag, first, last):
    q = s - lag
    if (q < 0 and first) or q >= QUADS:
        return None
    return q % QUADS, QUADS * g + q + 1


def count_of(g, s, lag):
    return (QUADS // 2) * g + (s - lag) // 2 + 1


def bank_tasks(first, last):
    k = QUADS // GI
    tasks = [(0, "K", 1), (1, "Q", 1), (3, "V", 1), (k, "K", 2), (k + 1, "Q", 2), (k + 3, "V", 2),
             (2 * k, "K", 3), (2 * k, "Q", 3), (2 * k + 3, "V", 3)]
    if not first:
        tasks += [(5, "Y", 0), (6, "Y", 1), (8, "Y", 2), (9, "Y", 3)]
    if not last:
        tasks += [(2 * k + 3, "XT", 0), (3 * k, "XT", 1), (3 * k, "XT", 2), (3 * k + 1, "XT", 3),
                  (3 * k + 1, "K", GI), (3 * k + 2, "Q", GI), (3 * k + 3, "V", GI)]
    else:
        tasks += [(QUADS + 3, "Y", 4 + j) for j in range(4)]
    return sorted(tasks, key=lambda task: task[0])


FIRST_TASKS = [("XT", 0), ("XT", 1), ("XT", 2), ("XT", 3), ("K", 0), ("Q", 0), ("V", 0)]
GROUP_TASKS = len(bank_tasks(False, False))
BEFORE_GROUP_1 = len(FIRST_TASKS) + len(bank_tasks(True, False))
ALL_TASKS = BEFORE_GROUP_1 + (GROUPS - 2) * GROUP_TASKS + len(bank_tasks(False, True))
assert GROUP_TASKS % 2 == 0


def place(task, groups=0):
    return task % 2, GROUP_TASKS // 2 * groups + task // 2


def tasks_of(g, first, last):
    start, groups = (len(FIRST_TASKS), 0) if first else (BEFORE_GROUP_1, g - 1)
    return [(s, kind, i, *place(start + t, groups))
            for t, (s, kind, i) in enumerate(bank_tasks(first, last))]


def places(g, first, last):
    if first:
        found = {task: place(t) for t, task in enumerate(FIRST_TASKS)}
    else:
        found = {(kind, i % GI): place(BEFORE_GROUP_1 - GROUP_TASKS + t, g - 1)
                 for t, (_, kind, i) in enumerate(bank_tasks(False, False)) if i == GI}
    return found | {(kind, i): (b, n) for _, kind, i, b, n in tasks_of(g, first, last)}


def over_groups(engine, group):
    group(0, 0, True, False)
    with engine.Fori(0, GROUPS // 2 - 1) as k:
        for par in (1, 0):
            group(2 * k + 2 - par, par, False, False)
    group(GROUPS - 1, 1, False, True)


PARAM_COLUMNS = [("wqkv", 3 * P), ("gain", 2), ("shift", 2), ("bqkv", 3), ("bf1", 2), ("bproj", C),
                 ("bf2", 1), ("rpb", HEADS * N), ("mask", 2 * P), ("wproj", P), ("w1", 2 * P),
                 ("w2", 2 * C), ("proj", C)]


def build(nc, x_d, params_d, out_d):
    with ExitStack() as ctx:
        def sb(name, *shape, dtype=F32):
            return ctx.enter_context(nc.sbuf_tensor(name, [P, *shape], dtype))

        def sem(name):
            return ctx.enter_context(nc.semaphore(name))

        bank = [ctx.enter_context(nc.psum_tensor(f"bank{i}", [P, BANK], F32)) for i in range(8)]

        x = sb("x", GROUPS * ROW)
        xn = sb("xn", ROW)
        xT = sb("xT", GI * IMG)
        qT = [sb(f"qT{i}", IMG) for i in range(2)]
        kT = [sb(f"kT{i}", IMG) for i in range(2)]
        kX = [sb(f"kX{i}", 2 * HEADS, IMG) for i in range(2)]
        vX = [sb(f"vX{i}", 4 * 2 * HEADS, 2 * HD) for i in range(2)]
        probs = [sb(f"probs{i}", BANK) for i in range(4)]
        probsT = [sb(f"probsT{i}", BANK) for i in range(2)]
        oT = [sb(f"oT{i}", GI * IMG) for i in range(2)]
        rT = [sb(f"rT{i}", P) for i in range(2)]
        recip = [sb(f"recip{i}", P) for i in range(4)]
        negmax = [sb(f"negmax{i}", 8) for i in range(4)]
        rowsum = [sb(f"rowsum{i}", 8) for i in range(4)]
        squares = [sb(f"squares{i}", PIECE) for i in range(2)]
        stat_sum = sb("stat_sum", SIDE)
        stat_mean = sb("stat_mean", SIDE)
        stat_sq = sb("stat_sq", SIDE)
        stat_var = sb("stat_var", SIDE)
        stat_rstd = sb("stat_rstd", SIDE)
        keys_mask = sb("keys_mask", 2 * HEADS)
        minus_half = sb("minus_half", SIDE)
        one_over_c = sb("one_over_c", SIDE)
        eps = sb("eps", SIDE)
        inverse = [sb(f"inverse{i}", 2 * HEADS) for i in range(4)]
        ident = sb("ident", P)
        v_bias = sb("v_bias", P)
        y_bias = sb("y_bias", C)
        bias = [sb(f"bias{i}", BANK) for i in range(2)]
        params = sb("params", sum(width for _, width in PARAM_COLUMNS))

        def param(name):
            at = 0
            for other, width in PARAM_COLUMNS:
                if other == name:
                    return params[:, at:at + width]
                at += width

        wraw = param("wqkv").rearrange("q (t o) -> q t o", t=3)
        w1raw = param("w1")
        w2 = param("w2").rearrange("q (t o) -> q t o", t=2)
        wproj, rpb, mask = param("wproj"), param("rpb"), param("mask")
        gain, shift, bqkv_raw, bf1_raw = (param(k) for k in ("gain", "shift", "bqkv", "bf1"))
        bproj, bf2, proj = param("bproj"), param("bf2"), param("proj")
        wqkv = sb("wqkv", 3, P)
        w1, w1_upper = sb("w1", FF), sb("w1_upper", FF)
        w1_hi, w1_lo = sb("w1_hi", FF, dtype=F32R), sb("w1_lo", FF, dtype=F32R)
        bqkv = sb("bqkv", 2)
        bf1 = sb("bf1", 2)
        xT2 = [sb(f"xT2_{i}", 2, BANK, dtype=F32R) for i in range(2)]
        upper = [xT[:, i * BANK:(i + 1) * BANK] for i in range(2)]
        hidden = [sb(f"hidden{i}", 4, BANK) for i in range(1)] + [kX[1][:, 0:4, :]]
        y2T = [sb(f"y2T{i}", BANK) for i in range(2)]

        scores = bank[0:2]
        trans = bank[2:4]
        outs = bank[4:6]
        work = bank[6:8]

        xT2_bank, fc1_bank, fc2_bank, y2_bank = bank[0:2], bank[2:6], bank[6], bank[7]

        x_loaded, params_in = sem("x_loaded"), sem("params_in")
        pool_ready, zeroed = sem("pool_ready"), sem("zeroed")
        params_ready, bias_made = sem("params_ready"), sem("bias_made")
        y_bias_summed, y_bias_made = sem("y_bias_summed"), sem("y_bias_made")
        w1_ready, biases_summed, keys_mask_made = (sem(k) for k in ("w1_ready", "biases_summed",
                                                                  "keys_mask_made"))
        scores_ready = [sem(f"scores_ready{i}") for i in range(2)]
        scores_taken = [sem(f"scores_taken{i}") for i in range(2)]
        negmax_ready = sem("negmax_ready")
        shifted = sem("shifted")
        probs_ready = sem("probs_ready")
        sum_ready, inverse_ready = sem("sum_ready"), sem("inverse_ready")
        recip_ready = sem("recip_ready")
        trans_ready = [sem(f"trans_ready{i}") for i in range(2)]
        trans_copied = [sem(f"trans_copied{i}") for i in range(2)]
        outs_ready = [sem(f"outs_ready{i}") for i in range(2)]
        rT_copied = [sem(f"rT_copied{i}") for i in range(2)]
        outs_taken = [sem(f"outs_taken{i}") for i in range(2)]
        work_ready = [sem(f"work_ready{i}") for i in range(2)]
        work_taken = [sem(f"work_taken{i}") for i in range(2)]
        kX_loaded = [sem(f"kX_loaded{i}") for i in range(2)]
        ln_sum, ln_mean, ln_centred = sem("ln_sum"), sem("ln_mean"), sem("ln_centred")
        ln_squares, ln_sq, ln_var = sem("ln_squares"), sem("ln_sq"), sem("ln_var")
        ln_rstd, xn_ready = sem("ln_rstd"), sem("xn_ready")
        xT2_ready, upper_ready = sem("xT2_ready"), sem("upper_ready")
        hi_copied, xT2_split = sem("hi_copied"), sem("xT2_split")
        fc1_ready, gelu_done = sem("fc1_ready"), sem("gelu_done")
        fc2_ready, y2T_copied = sem("fc2_ready"), sem("y2T_copied")
        y2_ready, out_ready, stored = sem("y2_ready"), sem("out_ready"), sem("stored")

        xn_v = xn[:, :].rearrange("q (p c w f) -> q p c w f", p=2, c=WIN, w=2)

        def first_half(G, i):
            before = (i - 1) % PIECES
            return (xn_v[:, before // 2, SHIFT:WIN, before % 2, :],
                    x[:, bass.ds(G * ROW + i * PIECE, SHIFT * C)], i * WIN, SHIFT)

        def second_half(G, i):
            return (xn_v[:, i // 2, 0:SHIFT, i % 2, :],
                    x[:, bass.ds(G * ROW + i * PIECE + SHIFT * C, SHIFT * C)], i * WIN + SHIFT, SHIFT)

        COPIES = 2 * GI
        KX_DMAS = 2 * HEADS
        KEYS_BY_ACT = 3

        S = GROUPS * PIECES

        block = ctx.enter_context(nc.Block())

        def rows_of(group_dma, g):
            for a in range(GI):
                for r0, r1, s0 in ((0, SIDE - SHIFT, SHIFT), (SIDE - SHIFT, SIDE, 0)):
                    hbm = group_dma[bass.ds(g * GI + a, 1), s0:s0 + r1 - r0]
                    yield (x[SIDE * a + r0:SIDE * a + r1, bass.ds(g * ROW, ROW)],
                           hbm.rearrange("o r c f -> (o r) (c f)"))

        @block.sync
        def _(sp):
            def load(g):
                for dst, src in rows_of(x_d, g):
                    sp.dma_start(dst, src).then_inc(x_loaded, 16)

            def spread_keys(par):
                for j in range(2 * HEADS):
                    rows = slice(HD * j, HD * (j + 1))
                    sp.dma_start(kX[par][rows, j, :], kT[par][rows, :]).then_inc(kX_loaded[par], 16)

            load(0)
            sp.dma_start(params[:, :], params_d).then_inc(params_in, 16)
            sp.wait_ge(x_loaded, 16 * COPIES)
            load(1)
            sp.wait_ge(zeroed, 2)

            def group(g, first, last, load_ahead):
                for s, kind, i, b, before in tasks_of(g, first, last):
                    if kind == "K":
                        sp.wait_ge(work_taken[b], before + 1)
                        spread_keys(i % 2)
                        if i == 1 and load_ahead:
                            sp.wait_ge(x_loaded, 16 * COPIES * (g + 2))
                            load(g + 2)

            group(0, True, False, True)
            with sp.Fori(1, GROUPS - 2) as g:
                group(g, False, False, True)
            group(GROUPS - 2, False, False, False)
            group(GROUPS - 1, False, True, False)

            with sp.Fori(0, GROUPS) as g:
                sp.wait_ge(out_ready, PIECES * g + PIECES)
                for src, dst in rows_of(out_d, g):
                    sp.dma_start(dst, src).then_inc(stored, 16)
            sp.wait_ge(stored, 16 * COPIES * GROUPS)

        @block.gpsimd
        def _(pool):
            nc.gpsimd.memset(minus_half[:, :], -0.5)
            nc.gpsimd.memset(one_over_c[:, :], 1.0 / C)
            nc.gpsimd.memset(eps[:, :], EPS)
            nc.gpsimd.memset(ident[:, :], 0.0).then_inc(pool_ready, 1)
            pool.wait_ge(pool_ready, 1)
            nc.gpsimd.affine_select(out=ident[:, :], in_=ident[:, :], compare_op=ALU.not_equal,
                                    fill=1.0, base=0, pattern=[[-1, P]], channel_multiplier=1)\
              .then_inc(pool_ready, 1)
            nc.gpsimd.memset(kX[1][:, :, :], 0.0).then_inc(zeroed, 1)

            def mean(n, u, cols):
                pool.wait_ge(ln_sum, u)
                nc.gpsimd.tensor_tensor(stat_mean[:, cols], stat_sum[:, cols], one_over_c[:, cols],
                                        ALU.mult).then_inc(ln_mean, 1)
                pool.wait_ge(ln_mean, n + 1)

            def rstd(n, u, cols):
                pool.wait_ge(ln_sq, u)
                nc.gpsimd.tensor_tensor(stat_var[:, cols], stat_sq[:, cols], eps[:, cols], ALU.add)\
                  .then_inc(ln_var, 1)
                pool.wait_ge(ln_var, n + 1)
                nc.gpsimd.tensor_tensor(stat_rstd[:, cols], stat_var[:, cols], minus_half[:, cols],
                                        ALU.pow).then_inc(ln_rstd, 1)
                pool.wait_ge(ln_rstd, n + 1)

            def centre(dst, src, c0, n):
                m = stat_mean[:, c0:c0 + n].unsqueeze(2).to_broadcast([P, n, C])
                return nc.gpsimd.tensor_tensor(dst, src.rearrange("q (a f) -> q a f", f=C), m, ALU.add)

            def scale(j):
                chunk = xn[:, j * PIECE:(j + 1) * PIECE].rearrange("q (a f) -> q a f", f=C)
                r = stat_rstd[:, j * WIN:(j + 1) * WIN].unsqueeze(2).to_broadcast([P, WIN, C])
                nc.gpsimd.tensor_tensor(chunk, chunk, r, ALU.mult).then_inc(xn_ready, 1)

            def centre_piece(G, i):
                centre(*first_half(G, i))
                centre(*second_half(G, i)).then_inc(ln_centred, 1)

            def centre2(s, r):
                cols = slice(r * WIN, (r + 1) * WIN)
                mean(GROUPS + s, S + s + 1, cols)
                if not isinstance(s, int) or s >= 4:
                    pool.wait_ge(xT2_ready, s - 3)
                centre(xn[:, r * PIECE:(r + 1) * PIECE].rearrange("q (a f) -> q a f", f=C),
                       x[:, bass.ds(s * PIECE, PIECE)], r * WIN, WIN).then_inc(ln_centred, 1)

            def chunk_cols(j):
                return slice(j * WIN, (j + 1) * WIN)

            every = slice(0, SIDE)
            mean(0, PIECES, every)
            centre_piece(0, 0)
            centre(*first_half(0, 1)).then_inc(ln_centred, 1)
            for j in range(PIECES):
                rstd(j, j + 1, chunk_cols(j))

            def add_y_bias(g, i):
                piece = x[:, bass.ds(g * ROW + i * PIECE, PIECE)].rearrange("q (a f) -> q a f", f=C)
                nc.gpsimd.tensor_tensor(piece, piece, y_bias[:, :].unsqueeze(1)
                                        .to_broadcast([P, WIN, C]), ALU.add)

            def group(g, par, first, last):
                for s in range(QUADS):
                    if s >= QUADS - PIECES:
                        if first and s == QUADS - PIECES:
                            pool.wait_ge(y_bias_made, 1)
                        add_y_bias(g, s - (QUADS - PIECES))
                    pool.wait_ge(negmax_ready, QUADS * g + s + 1)
                    top = negmax[s % 4][:, :].unsqueeze(2).to_broadcast([P, 8, N])
                    e = probs[s % 4][:, :].rearrange("q (a m) -> q a m", m=N)
                    nc.gpsimd.tensor_tensor(e, e, top, ALU.add).then_inc(shifted, 1)
                    u = PIECES * (g + 1)
                    for i in ln_pieces("centre", s):
                        if last:
                            centre2(i, i)
                            continue
                        if i == 0:
                            mean(g + 1, u + PIECES, every)
                        centre_piece(g + 1, i)
                    for j in ln_pieces("rstd", s):
                        rstd(u + j, u + j + 1, chunk_cols(j))
                    for j in ln_pieces("scale", s):
                        scale(j)

            over_groups(pool, group)

            def scale2(s, r):
                rstd(S + s, S + s + 1, chunk_cols(r))
                scale(r)

            for s in range(4):
                if s >= 2:
                    scale2(s + 2, (s + 2) % 4)
                centre2(s + 4, s)
            with pool.Fori(1, S // 4 - 1) as k:
                for d in range(4):
                    scale2(4 * k + d + 2, (d + 2) % 4)
                    centre2(4 * k + d + 4, d)
            for s in range(S - 4, S - 2):
                scale2(s + 2, (s + 2) % 4)

        @block.vector
        def _(dve):
            def row_sum(src, cols, n, u):
                if not isinstance(n, int) or n:
                    dve.wait_ge(ln_mean, n)
                nc.vector.tensor_reduce(stat_sum[:, cols], src.rearrange("q (a f) -> q a f", f=C), AXX,
                                        ALU.add, negate=True).then_inc(ln_sum, 1)

            def square_sum(j, r, u):
                dve.wait_ge(ln_squares, u + 1)
                nc.vector.tensor_reduce(stat_sq[:, r * WIN:(r + 1) * WIN],
                                        squares[j % 2][:, :].rearrange("q (a f) -> q a f", f=C),
                                        AXX, ALU.add).then_inc(ln_sq, 1)

            nc.vector.memset(vX[0][:, :, :], 0.0)
            nc.vector.memset(vX[1][:, :, :], 0.0).then_inc(zeroed, 1)
            for b in range(2):
                dve.sem_inc(scores_taken[b], 1)
                dve.sem_inc(outs_taken[b], 1)
            dve.wait_ge(x_loaded, 16 * COPIES)
            for i in range(PIECES):
                row_sum(x[:, i * PIECE:(i + 1) * PIECE], slice(i * WIN, (i + 1) * WIN), 0, i)
            dve.wait_ge(ln_mean, 1)
            for half, i in ((second_half, 1), (first_half, 2), (second_half, 2), (first_half, 3),
                            (second_half, 3)):
                dst, src, c0, n = half(0, i)
                done = nc.vector.tensor_tensor(
                    dst, src.rearrange("q (a f) -> q a f", f=C),
                    stat_mean[:, c0:c0 + n].unsqueeze(2).to_broadcast([P, n, C]), ALU.add)
                if half == second_half and i > 1:
                    done.then_inc(ln_centred, 1)
            dve.wait_ge(params_in, 16)
            for t in range(3):
                last = nc.vector.tensor_scalar(wqkv[:, t, :], wraw[:, t, :], gain[:, 0:1], None,
                                               ALU.mult)
            last.then_inc(params_ready, 1)
            for j in range(PIECES):
                square_sum(j, j, j)
            dve.wait_ge(pool_ready, 2)
            nc.vector.tensor_reduce(keys_mask[:, :], ident[:, :].rearrange("q (j d) -> q j d", d=HD),
                                    AXX, ALU.add).then_inc(keys_mask_made, 1)
            dve.wait_ge(y_bias_summed, 1)
            nc.vector.tensor_tensor(y_bias[:, :], outs[1][:, 0:C], bproj[:, :], ALU.add)\
              .then_inc(y_bias_made, 1)
            for j in range(PIECES):
                dve.wait_ge(ln_rstd, j + 1)
                chunk = xn[:, j * PIECE:(j + 1) * PIECE].rearrange("q (a f) -> q a f", f=C)
                r = stat_rstd[:, j * WIN:(j + 1) * WIN].unsqueeze(2).to_broadcast([P, WIN, C])
                nc.vector.tensor_tensor(chunk, chunk, r, ALU.mult).then_inc(xn_ready, 1)
                if j >= 2:
                    continue
                r = rpb[:, :].rearrange("q (h m) -> q h m", h=HEADS).unsqueeze(2)\
                    .to_broadcast([P, HEADS, 2, N])
                m = mask[:, j * P:(j + 1) * P].rearrange("q (p m) -> q p m", p=2).unsqueeze(1)\
                    .to_broadcast([P, HEADS, 2, N])
                nc.vector.tensor_tensor(bias[j][:, :].rearrange("q (h p m) -> q h p m", h=HEADS, p=2),
                                        r, m, ALU.add).then_inc(bias_made, 1)
            dve.wait_ge(keys_mask_made, 1)
            b, before = places(0, True, False)["K", 0]
            dve.wait_ge(work_taken[b], before + 1)
            for j in range(KEYS_BY_ACT, 2 * HEADS):
                nc.vector.tensor_scalar(kX[0][:, j, :], kT[0][:, :], keys_mask[:, j:j + 1], None,
                                        ALU.mult).then_inc(kX_loaded[0], 16)
            nc.vector.tensor_scalar(w1[:, :], w1raw[:, :], gain[:, 1:2], None, ALU.mult)\
              .then_inc(w1_ready, 1)
            dve.wait_ge(w1_ready, 1)
            nc.vector.tensor_scalar(w1_upper[:, :].bitcast(I32), w1[:, :].bitcast(I32), UPPER, None,
                                    ALU.bitwise_and).then_inc(w1_ready, 1)
            dve.wait_ge(w1_ready, 2)
            nc.vector.tensor_copy(w1_hi[:, :], w1_upper[:, :])
            nc.vector.tensor_tensor(w1_lo[:, :], w1[:, :], w1_upper[:, :], ALU.subtract)\
              .then_inc(w1_ready, 1)
            dve.wait_ge(bias_made, 2)

            def sum2(s, r):
                row_sum(x[:, bass.ds(s * PIECE, PIECE)], slice(r * WIN, (r + 1) * WIN),
                        GROUPS + (s - 3 if not isinstance(s, int) or s > 3 else 0), S + s)

            def split(s, par):
                dve.wait_ge(xT2_ready, s + 1)
                if not isinstance(s, int) or s >= 2:
                    dve.wait_ge(fc1_ready, 4 * s - 4)
                    dve.wait_ge(hi_copied, s - 1)
                src = xT2_bank[par]
                nc.vector.tensor_scalar(upper[par].bitcast(I32), src[:, :].bitcast(I32), UPPER, None,
                                        ALU.bitwise_and).then_inc(upper_ready, 1)
                dve.wait_ge(upper_ready, s + 1)
                nc.vector.tensor_copy(xT2[par][C:P, 1, :], upper[par][C:P, :])
                for w, rows, other in ((0, slice(0, C), slice(C, P)), (1, slice(C, P), slice(0, C))):
                    done = nc.vector.tensor_tensor(xT2[par][other, w, :], src[rows, :],
                                                   upper[par][rows, :], ALU.subtract)
                done.then_inc(xT2_split, 1)

            def group(g, par, first, last):
                tasks = tasks_of(g, first, last)
                for s in group_slots(last):
                    if last and s == QUADS:
                        split(0, 0)
                    if last and s == QUADS + 3:
                        split(1, 1)
                        sum2(4, 0)
                    if s < QUADS:
                        b, fill = s % 2, (QUADS // 2) * g + s // 2
                        e = probs[s % 4]
                        dve.wait_ge(scores_ready[b], fill + 1)
                        nc.vector.tensor_tensor(e[:, :], scores[b][:, :],
                                                bias[s % 4 == 3][:, :], ALU.add)\
                          .then_inc(scores_taken[b], 1)
                        dve.wait_ge(scores_taken[b], fill + 2)
                        e3 = e[:, :].rearrange("q (a m) -> q a m", m=N)
                        nc.vector.tensor_reduce(negmax[s % 4][:, :], e3, AXX, ALU.max, negate=True)\
                          .then_inc(negmax_ready, 1)
                    if at := at_lag(g, s, 1, first, last):
                        q, n = at
                        dve.wait_ge(probs_ready, n)
                        nc.vector.tensor_reduce(rowsum[q % 4][:, :],
                                                probs[q % 4][:, :].rearrange("q (a m) -> q a m", m=N),
                                                AXX, ALU.add).then_inc(sum_ready, 1)
                    if at := at_lag(g, s, PV_LAG, first, last):
                        q, n = at
                        b = q % 2
                        dve.wait_ge(rT_copied[b], count_of(g, s, PV_LAG))
                        own = par if s >= PV_LAG else 1 - par
                        dst = oT[own][:, :].rearrange("q (w c i y r) -> q i y w r c", w=2, c=WIN,
                                                      i=GI, y=SIDE // WIN)[:, q // 4, q % 4]
                        o, r = (t[:, 0:P].rearrange("q (w r c) -> q w r c", w=2, r=WIN)
                                for t in (outs[b], rT[b]))
                        nc.vector.tensor_tensor(dst, o, r, ALU.mult)\
                          .then_inc(outs_taken[b], 1)
                    if at := at_lag(g, s, 1, first, last):
                        q, n = at
                        dve.wait_ge(sum_ready, n)
                        nc.vector.reciprocal(inverse[q % 4][:, :], rowsum[q % 4][:, :])\
                          .then_inc(inverse_ready, 1)
                    for i in ln_pieces("sum", s):
                        if last:
                            sum2(i, i)
                            continue
                        if i == 0:
                            dve.wait_ge(x_loaded, 16 * COPIES * (g + 2))
                        row_sum(x[:, bass.ds((g + 1) * ROW + i * PIECE, PIECE)],
                                slice(i * WIN, (i + 1) * WIN), g + 1, PIECES * (g + 1) + i)
                    for j in ln_pieces("square_sum", s):
                        square_sum(j, j, PIECES * (g + 1) + j)
                    for ts, kind, j, b, fill in tasks:
                        if ts != s or kind != "Y":
                            continue
                        dve.wait_ge(work_ready[b], fill + 1)
                        G = g if j >= 4 else g - 1
                        j %= 4
                        w, c0 = j // 2, (j % 2) * SHIFT
                        src = work[b][:, :].rearrange("q (c p f) -> q c p f", c=4, p=2)
                        if (w, c0) != (1, SHIFT):
                            col = WIN * w + c0 + SHIFT
                            dst = x[:, bass.ds(G * ROW, ROW)]\
                                .rearrange("q (p c f) -> q c p f", p=2, f=C)[:, col:col + SHIFT]
                            nc.vector.tensor_tensor(dst, src, dst, ALU.add)\
                              .then_inc(work_taken[b], 1)
                            continue
                        for p, col in ((0, 2 * WIN), (1, 0)):
                            dst = x[:, bass.ds(G * ROW + col * C, SHIFT * C)]\
                                .rearrange("q (c f) -> q c f", f=C)
                            done = nc.vector.tensor_tensor(dst, src[:, :, p, :], dst, ALU.add)
                        done.then_inc(work_taken[b], 1)

            over_groups(dve, group)
            for b in range(2):
                dve.wait_ge(work_taken[b], (ALL_TASKS + 1 - b) // 2)

            def step(s, d, sums, parts, squares_sum, add):
                if sums:
                    sum2(s + 4, d)
                if parts:
                    split(s + 1, (d + 1) % 2)
                if squares_sum:
                    square_sum((d + 3) % 4, (d + 3) % 4, S + s + 3)
                if add:
                    dve.wait_ge(y2_ready, s - 1)
                    dst = x[:, bass.ds((s - 2) * PIECE, PIECE)]
                    nc.vector.tensor_tensor(dst, y2_bank[:, :], dst, ALU.add).then_inc(out_ready, 1)

            for s in range(1, 4):
                step(s, s, True, True, True, s >= 2)
            with dve.Fori(1, S // 4 - 1) as k:
                for d in range(4):
                    step(4 * k + d, d, True, True, True, True)
            for s in range(S - 4, S + 2):
                step(s, s % 4, False, s + 1 < S, s + 3 < S, True)

        @block.scalar
        def _(act):
            def square(j, r, u, centred_u):
                act.wait_ge(ln_centred, centred_u)
                if not isinstance(u, int) or u >= 2:
                    act.wait_ge(ln_sq, u - 1)
                nc.scalar.activation(squares[j % 2][:, :], xn[:, r * PIECE:(r + 1) * PIECE], ACT.Square,
                                     scale=float(C) ** -0.5).then_inc(ln_squares, 1)

            def take(kind, i, b, fill):
                act.wait_ge(work_ready[b], fill + 1)
                src, par = work[b], i % 2
                if kind == "XT":
                    p, c0 = i // 2, i % 2 * 4
                    dst = xT[:, :].rearrange("q (i p r c) -> q p c i r", p=2, r=WIN, c=WIN)
                    done = nc.scalar.activation(
                        dst[:, p, c0:c0 + 4],
                        src[:, :].rearrange("q (c i r) -> q c i r", c=4, r=WIN), ACT.Copy)
                elif kind == "Q":
                    done = nc.scalar.activation(qT[par][:, :], src[:, :], ACT.Identity,
                                                bias=bqkv[:, 0:1], scale=float(HD) ** -0.5)
                elif kind == "K":
                    done = nc.scalar.activation(kT[par][:, :], src[:, :], ACT.Identity,
                                                bias=bqkv[:, 1:2])
                elif kind == "V":
                    for p in range(2):
                        half = slice(N * p, N * (p + 1))
                        done = nc.scalar.activation(
                            vX[par][half, :, HD * p:HD * (p + 1)],
                            src[half, :].rearrange("q (a d) -> q a d", d=HD), ACT.Copy)
                done.then_inc(work_taken[b], 1)

            for j in range(PIECES):
                square(j, j, j, PIECES)
            act.wait_ge(biases_summed, 1)
            scale = float(HD) ** -0.5
            nc.scalar.activation(bqkv[:, 1:2], bank[0][:, 1:2], ACT.Copy).then_inc(params_ready, 1)
            nc.scalar.activation(v_bias[:, :], bank[0][:, 2:3].to_broadcast([P, P]), ACT.Copy)\
              .then_inc(params_ready, 1)
            nc.scalar.activation(bqkv[:, 0:1], bank[0][:, 0:1], ACT.Copy, scale=scale)\
              .then_inc(params_ready, 1)
            nc.scalar.activation(bf1[:, :], bank[0][:, 3:5], ACT.Copy).then_inc(params_ready, 1)
            for t, (kind, i) in enumerate(FIRST_TASKS):
                b, before = place(t)
                take(kind, i, b, before)
                if kind == "K":
                    act.wait_ge(keys_mask_made, 1)
                    act.wait_ge(work_taken[b], before + 1)
                    for j in range(KEYS_BY_ACT):
                        nc.scalar.activation(kX[0][:, j, :], kT[0][:, :], ACT.Copy,
                                             scale=keys_mask[:, j:j + 1]).then_inc(kX_loaded[0], 16)

            def square2(s, r):
                square(r, r, S + s, S + s + 1)

            def copy_hi(s, par):
                act.wait_ge(upper_ready, s + 1)
                nc.scalar.activation(xT2[par][0:C, 0, :], upper[par][0:C, :], ACT.Copy)\
                  .then_inc(hi_copied, 1)

            def group(g, par, first, last):
                tasks = tasks_of(g, first, last)
                for s in group_slots(last):
                    if last and s == QUADS + 2:
                        copy_hi(0, 0)
                    for ts, kind, i, b, fill in tasks:
                        if ts == s and kind != "Y":
                            take(kind, i, b, fill)
                    if at := at_lag(g, s, 1, first, last):
                        q, n = at
                        act.wait_ge(shifted, n)
                        nc.scalar.activation(probs[q % 4][:, :], probs[q % 4][:, :], ACT.Exp)\
                          .then_inc(probs_ready, 1)
                    if at := at_lag(g, s, TR_LAG, first, last):
                        q, n = at
                        b = q % 2
                        act.wait_ge(trans_ready[b], count_of(g, s, TR_LAG))
                        nc.scalar.activation(probsT[b][:, :], trans[b][:, :], ACT.Copy)\
                          .then_inc(trans_copied[b], 1)
                        act.wait_ge(inverse_ready, n)
                        nc.scalar.activation(recip[q % 4][:, :].rearrange("q (a d) -> q a d", d=HD),
                                             inverse[q % 4][:, :].unsqueeze(2)
                                             .to_broadcast([P, 2 * HEADS, HD]), ACT.Copy)\
                          .then_inc(recip_ready, 1)
                    if at := at_lag(g, s, PV_LAG, first, last):
                        b = at[0] % 2
                        act.wait_ge(outs_ready[b], count_of(g, s, PV_LAG))
                        nc.scalar.activation(rT[b][:, :], outs[b][:, P:2 * P], ACT.Copy)\
                          .then_inc(rT_copied[b], 1)
                    for j in ln_pieces("square", s):
                        if last:
                            square2(j, j)
                            continue
                        square(j, j, PIECES * (g + 1) + j,
                               PIECES * (g + 1) + (PIECES if j == 3 else j + 2))

            over_groups(act, group)
            copy_hi(1, 1)

            def step(s, d, hid, hi, ahead, out):
                par = d % 2
                if hid:
                    for j in range(4):
                        act.wait_ge(fc1_ready, 4 * s + j + 1)
                        nc.scalar.activation(hidden[par][:, j, :], fc1_bank[j][:, :],
                                             ACT.Gelu_apprx_tanh, bias=bf1[:, j % 2:j % 2 + 1])\
                          .then_inc(gelu_done, 1)
                if hi:
                    copy_hi(s + 1, 1 - par)
                if ahead:
                    square2(s + 3, (d + 3) % 4)
                if out:
                    act.wait_ge(fc2_ready, s)
                    nc.scalar.activation(y2T[1 - par][:, :], fc2_bank[:, :], ACT.Identity,
                                         bias=bf2[:, 0:1]).then_inc(y2T_copied, 1)

            for s in range(4):
                step(s, s, True, s >= 1, s >= 1, s >= 1)
            with act.Fori(1, S // 4 - 1) as k:
                for d in range(4):
                    step(4 * k + d, d, True, True, True, True)
            for s in range(S - 4, S + 1):
                step(s, s % 4, s < S, s + 1 < S, s + 3 < S, True)

        @block.tensor
        def _(pe):
            def mm(out, lhsT, rhs, start=True, stop=True):
                return nc.tensor.matmul(out, lhsT, rhs, start=start, stop=stop)

            def fill(kind, i, b, before, group_par=0):
                if not isinstance(before, int) or before:
                    pe.wait_ge(work_taken[b], before)
                out = work[b]
                if kind == "XT":
                    for k in range(4):
                        jj = 4 * i + k
                        done = nc.tensor.transpose(out[:, k * P:(k + 1) * P],
                                                   xn[:, jj * P:(jj + 1) * P], ident[:, :])
                elif kind in ("Q", "K"):
                    done = mm(out[:, :], wqkv[:, "QKV".index(kind), :],
                              xT[:, i % GI * IMG:(i % GI + 1) * IMG])
                elif kind == "V":
                    for k in range(4):
                        at = i % GI * IMG + k * P
                        done = mm(out[:, k * P:(k + 1) * P], xT[:, at:at + P], wqkv[:, 2, :])
                elif kind == "Y":
                    for k in range(4):
                        jj = 4 * (i % 4) + k
                        done = mm(out[:, k * P:(k + 1) * P], oT[group_par][:, jj * P:(jj + 1) * P],
                                  wproj[:, :])
                done.then_inc(work_ready[b], 1)

            pe.wait_ge(params_in, 16)
            pe.wait_ge(pool_ready, 2)
            for t in range(3):
                mm(bank[0][:, t:t + 1], wraw[:, t, :], shift[:, 0:1], stop=False)
                mm(bank[0][:, t:t + 1], ident[:, :], bqkv_raw[:, t:t + 1], start=False)
            for t in range(2):
                mm(bank[0][:, 3 + t:4 + t], w1raw[0:C, t * P:(t + 1) * P], shift[0:C, 1:2], stop=False)
                done = mm(bank[0][:, 3 + t:4 + t], ident[:, :], bf1_raw[:, t:t + 1], start=False)
            done.then_inc(biases_summed, 1)

            def warm(n):
                for _ in range(n):
                    mm(trans[0][:, :], ident[:, :], params[:, 0:BANK])

            pe.wait_ge(params_ready, 5)
            mm(outs[1][:, 0:C], v_bias[:, :], proj[:, :]).then_inc(y_bias_summed, 1)
            for t, (kind, i) in enumerate(FIRST_TASKS):
                if kind == "K":
                    pe.wait_ge(work_taken[1], t // 2)
                if kind == "XT":
                    warm(2 if i == 0 else 1)
                    pe.wait_ge(xn_ready, i + 1)
                fill(kind, i, *place(t))
            pe.wait_ge(zeroed, 2)
            pe.wait_ge(y_bias_made, 1)

            def transpose_piece(s, d):
                pe.wait_ge(xn_ready, S + s + 1)
                if not isinstance(s, int) or s >= 2:
                    pe.wait_ge(xT2_split, s - 1)
                for k in range(4):
                    at = d * PIECE + k * P
                    done = nc.tensor.transpose(xT2_bank[d % 2][:, k * P:(k + 1) * P],
                                               xn[:, at:at + P], ident[:, :])
                done.then_inc(xT2_ready, 1)

            def fc1(s, par, banks=range(4)):
                for j in banks:
                    w, half = j // 2, j % 2
                    if j == 0:
                        pe.wait_ge(xT2_split, s + 1)
                        pe.wait_ge(hi_copied, s + 1)
                    if not isinstance(s, int) or s:
                        pe.wait_ge(gelu_done, 4 * s + j - 3)
                    cols = slice(half * P, (half + 1) * P)
                    mm(fc1_bank[j][:, :], w1_hi[:, cols], xT2[par][:, w, :], stop=False)
                    mm(fc1_bank[j][:, :], w1_lo[:, cols], xT2[par][:, w, :], start=False)\
                        .then_inc(fc1_ready, 1)

            def group(g, par, first, last):
                tasks = tasks_of(g, first, last)
                at_place = places(g, first, last)

                def copied(kind, i):
                    b, before = at_place[kind, i]
                    pe.wait_ge(work_taken[b], before + 1)

                for s in group_slots(last):
                    if last and s in (QUADS, QUADS + 1):
                        pe.wait_ge(scores_taken[s % 2], (QUADS // 2) * GROUPS + 1)
                        transpose_piece(s - QUADS, s - QUADS)
                    if last and s == QUADS + 3:
                        pe.wait_ge(w1_ready, 3)
                        for b in range(2):
                            pe.wait_ge(trans_copied[b], (QUADS // 2) * GROUPS)
                        fc1(0, 0, (0, 1))
                        for b in range(2):
                            pe.wait_ge(outs_taken[b], (QUADS // 2) * GROUPS + 1)
                        fc1(0, 0, (2, 3))
                    if s < QUADS:
                        image, wi = divmod(s, 4)
                        two, b, before = image % 2, s % 2, (QUADS // 2) * g + s // 2
                        if wi == 0:
                            pe.wait_ge(kX_loaded[two], 16 * KX_DMAS * (2 * g + image // 2 + 1))
                            copied("Q", image)
                        pe.wait_ge(scores_taken[b], before + 1)
                        for p in range(2):
                            at = wi * P + p * N
                            for w in range(2):
                                out = scores[b][w * N:(w + 1) * N, :]\
                                    .rearrange("q (h p m) -> q p h m", h=HEADS, p=2)[:, p]
                                done = mm(out, qT[two][:, at:at + N],
                                          kX[two][:, HEADS * w:HEADS * (w + 1), at:at + N])
                        done.then_inc(scores_ready[b], 1)
                    for ts, kind, i, b, before in tasks:
                        if ts != s or kind == "Y":
                            continue
                        if kind == "K" and i == GI:
                            copied("XT", 2)
                            copied("XT", 3)
                        if kind == "XT":
                            pe.wait_ge(xn_ready, PIECES * (g + 1) + i + 1)
                        fill(kind, i, b, before)
                    if at := at_lag(g, s, TR_LAG, first, last):
                        q, n = at
                        b = q % 2
                        pe.wait_ge(probs_ready, n)
                        for h in range(HEADS):
                            done = nc.tensor.transpose(trans[b][:, h * P:(h + 1) * P],
                                                       probs[q % 4][:, h * P:(h + 1) * P], ident[:, :])
                        done.then_inc(trans_ready[b], 1)
                    if at := at_lag(g, s, PV_LAG, first, last):
                        q, n = at
                        image, wi = divmod(q, 4)
                        b, count = q % 2, count_of(g, s, PV_LAG)
                        if wi == 0:
                            copied("V", image)
                        pe.wait_ge(trans_copied[b], count)
                        pe.wait_ge(outs_taken[b], count)
                        for w in range(2):
                            for h in range(HEADS):
                                mm(outs[b][2 * HD * h:2 * HD * (h + 1), w * N:(w + 1) * N],
                                   vX[image % 2][:, (wi * 2 + w) * HEADS + h, :],
                                   probsT[b][:, (2 * h + w) * N:(2 * h + w + 1) * N])
                        pe.wait_ge(recip_ready, n)
                        nc.tensor.transpose(outs[b][:, P:2 * P], recip[q % 4][:, :], ident[:, :])\
                          .then_inc(outs_ready[b], 1)
                    for ts, kind, i, b, before in tasks:
                        if ts != s or kind != "Y":
                            continue
                        if i % 4 == 0:
                            for o in range(2):
                                pe.wait_ge(outs_taken[o], (QUADS // 2) * (g + i // 4) + 1)
                        fill(kind, i, b, before, par if i >= 4 else 1 - par)

            over_groups(pe, group)

            for b in range(2):
                pe.wait_ge(work_taken[b], (ALL_TASKS + 1 - b) // 2)

            def step(s, d, f1, xt, f2, y):
                par = d % 2
                if xt:
                    transpose_piece(s + 1, (d + 1) % 4)
                if f1:
                    fc1(s, par)
                if f2:
                    pe.wait_ge(gelu_done, 4 * s)
                    if not isinstance(s, int) or s >= 2:
                        pe.wait_ge(y2T_copied, s - 1)
                    for half in range(2):
                        for w in range(2):
                            done = mm(fc2_bank[C * w:C * (w + 1), :], w2[:, half, :],
                                      hidden[1 - par][:, 2 * w + half, :], start=half == 0,
                                      stop=half == 1)
                    done.then_inc(fc2_ready, 1)
                if y:
                    pe.wait_ge(y2T_copied, s - 1)
                    if not isinstance(s, int) or s >= 3:
                        pe.wait_ge(out_ready, s - 2)
                    for k in range(4):
                        done = nc.tensor.transpose(y2_bank[:, k * P:(k + 1) * P],
                                                   y2T[par][:, k * P:(k + 1) * P], ident[:, :])
                    done.then_inc(y2_ready, 1)

            for s in range(4):
                step(s, s, s >= 1, s >= 1, s >= 1, s >= 2)
            with pe.Fori(1, S // 4 - 1) as k:
                for d in range(4):
                    step(4 * k + d, d, True, True, True, True)
            for s in range(S - 4, S + 2):
                step(s, s % 4, s < S, s + 1 < S, s <= S, True)


def pack_params(ln1_g, ln1_b, qkv_w, qkv_b, proj_w, proj_b, rpb, ln2_g, ln2_b, fc1_w, fc1_b, fc2_w,
                fc2_b):
    def twice(a):
        return np.concatenate([a, a])

    wqkv = np.zeros((2, C, 3, 2, C), np.float32)
    wproj = np.zeros((HEADS, 2, HD, 2, C), np.float32)
    for k in range(2):
        wqkv[k, :, :, k] = qkv_w.reshape(C, 3, C)
        wproj[:, k, :, k] = proj_w.reshape(HEADS, HD, C)
    columns = {
        "wqkv": wqkv.reshape(P, 3 * P), "w1": twice(fc1_w), "wproj": wproj.reshape(P, P),
        "w2": fc2_w.reshape(2, P, C).transpose(1, 0, 2).reshape(P, 2 * C),
        "gain": twice(np.stack([ln1_g, ln2_g], 1)), "shift": twice(np.stack([ln1_b, ln2_b], 1)),
        "bqkv": twice(qkv_b.reshape(3, C).T), "bf1": fc1_b.reshape(2, P).T,
        "bproj": np.tile(proj_b, (P, 1)), "bf2": twice(fc2_b[:, None]),
        "rpb": twice(rpb[rel_pos_index()].transpose(0, 2, 1).reshape(N, HEADS * N)),
        "mask": shift_masks(), "proj": np.concatenate([proj_w, np.zeros((C, C), np.float32)]),
    }
    return np.ascontiguousarray(np.concatenate([columns[name] for name, _ in PARAM_COLUMNS], 1))


def kernel(**inputs):
    import concourse.bacc as bacc
    from concourse.bass_utils import run_bass_kernel_spmd

    x = np.ascontiguousarray(inputs["x"])
    params = pack_params(**{name.removeprefix("L0_conv_"): np.asarray(a)
                            for name, a in inputs.items() if name != "x"})
    nc = bacc.Bacc("TRN2", target_bir_lowering=False, num_devices=1)
    x_d = nc.dram_tensor("in_x", x.shape, F32, kind="ExternalInput").ap()
    params_d = nc.dram_tensor("in_params", params.shape, F32, kind="ExternalInput").ap()
    out_d = nc.dram_tensor("out", x.shape, F32, kind="ExternalOutput").ap()
    build(nc, x_d, params_d, out_d)
    r = run_bass_kernel_spmd(nc, [{"in_x": x, "in_params": params}], core_ids=[0])
    return r.results[0]["out"]
```
